# Optimizing a Trainium2 kernel written in Bass

```python
import numpy as np
import jax
import jax.numpy as jnp

def _softmax(x, axis=-1):
    return jax.nn.softmax(x, axis=axis)

def _gelu(x):
    return jax.nn.gelu(x, approximate=True)

def _silu(x):
    return jax.nn.silu(x)

def _sigmoid(x):
    return jax.nn.sigmoid(x)

def _layernorm(x, axis=-1, eps=1e-05):
    m = jnp.mean(x, axis=axis, keepdims=True)
    v = jnp.var(x, axis=axis, keepdims=True)
    return (x - m) / jnp.sqrt(v + eps)

def _scatter_add(tgt, idx, src, axis=0):
    return tgt.at[idx].add(src)

def _segment_sum(src, seg, n):
    return jax.ops.segment_sum(src, seg, n)
kernel_name = 'mk_flamingo_gated_d1_seqx_r4_173a1c'

def setup_inputs(seed: int=0):
    np.random.seed(seed)
    _w = jnp.asarray

    def _rec_inputs():
        import jax
        import jax.numpy as jnp
        _rk = jax.random.key(seed)
        x = 7.22e-05 + 1 * jax.random.normal(jax.random.fold_in(_rk, 1), (2, 1024, 256), jnp.float32)
        _lenS = 1024 - jax.random.randint(jax.random.fold_in(_rk, 7), (2,), 0, max(1, 1024 // 4) + 1, jnp.int32)
        _lenS2 = 154 - jax.random.randint(jax.random.fold_in(_rk, 8), (2,), 0, max(1, 154 // 4) + 1, jnp.int32)
        _ctx_1024P = jax.random.normal(jax.random.fold_in(_rk, 11), (2, 16, 256), jnp.float32)
        _ctx_1024c = jax.random.dirichlet(jax.random.fold_in(_rk, 511), 0.3 * jnp.ones((16,), jnp.float32), (2, 154))
        _ctx_1024t = jnp.einsum('bsk,bkd->bsd', _ctx_1024c, _ctx_1024P)
        _ctx_1024t = _ctx_1024t * jax.lax.rsqrt(jnp.mean(jnp.square(_ctx_1024t)) + 1e-12) * 0.953939
        ctx_1024 = 4.13588e-05 + 0.999923 * (_ctx_1024t + 0.3 * jax.random.normal(jax.random.fold_in(_rk, 611), (2, 154, 256), jnp.float32))
        _validS = jnp.arange(1024)[None, :] < _lenS[:, None]
        _validS2 = jnp.arange(154)[None, :] < _lenS2[:, None]
        _causal = jnp.tril(jnp.ones((1024, 1024), dtype=bool))
        mask_BxS2_bf1 = jnp.ones((2, 154), dtype=bool)
        _g = jax.random.normal(jax.random.fold_in(_rk, 9001), (2, 1), jnp.float32)
        _g = jnp.sign(_g) * jnp.maximum(jnp.abs(_g), 1.0) + (_g == 0) * 1.0
        g_xattn = _g[0]
        g_ffn = _g[1]
        return (x, ctx_1024, mask_BxS2_bf1, g_xattn, g_ffn)
    x, ctx_1024, mask_BxS2_bf1, g_xattn, g_ffn = _rec_inputs()

    def _L0_xattn_setup():
        import jax, jax.numpy as jnp
        import numpy as np
        D_MODEL = 256
        N_HEADS = 16
        HEAD_DIM = D_MODEL // N_HEADS
        key = jax.random.key(seed)
        ks = jax.random.split(key, 11)
        B, Q, K = (4, 512, 512)
        s = 1.0 / np.sqrt(D_MODEL)
        inp = {'q': jax.random.normal(ks[0], (B, Q, D_MODEL), jnp.float32), 'k': jax.random.normal(ks[1], (B, K, D_MODEL), jnp.float32), 'v': jax.random.normal(ks[2], (B, K, D_MODEL), jnp.float32), 'kv_mask': jnp.ones((B, K), dtype=bool), 'Wq': jax.random.normal(ks[3], (D_MODEL, D_MODEL), jnp.float32) * s, 'bq': jnp.zeros((D_MODEL,), jnp.float32), 'Wk': jax.random.normal(ks[4], (D_MODEL, D_MODEL), jnp.float32) * s, 'bk': jnp.zeros((D_MODEL,), jnp.float32), 'Wv': jax.random.normal(ks[5], (D_MODEL, D_MODEL), jnp.float32) * s, 'bv': jnp.zeros((D_MODEL,), jnp.float32), 'Wo': jax.random.normal(ks[6], (D_MODEL, D_MODEL), jnp.float32) * s, 'bo': jnp.zeros((D_MODEL,), jnp.float32)}
        return inp
    _L0_xattn_all = _L0_xattn_setup()
    _L0_xattn_in = {k: v for k, v in _L0_xattn_all.items() if k in ('Wq', 'bq', 'Wk', 'bk', 'Wv', 'bv', 'Wo', 'bo')}
    del _L0_xattn_all

    def _L0_ffn_setup():
        import jax, jax.numpy as jnp
        import numpy as np
        TOP_K = 2
        key = jax.random.key(seed)
        ks = jax.random.split(key, 6)
        B, L, D, E, F = (2, 512, 256, 8, 1024)
        x = jax.random.normal(ks[0], (B, L, D), dtype=jnp.float32)
        Wg = jax.random.normal(ks[1], (D, E), dtype=jnp.float32) * D ** (-0.5)
        W1 = jax.random.normal(ks[2], (E, D, F), dtype=jnp.float32) * D ** (-0.5)
        b1 = jnp.zeros((E, F), dtype=jnp.float32)
        W2 = jax.random.normal(ks[3], (E, F, D), dtype=jnp.float32) * F ** (-0.5)
        b2 = jnp.zeros((E, D), dtype=jnp.float32)
        return {'x': x, 'Wg': Wg, 'W1': W1, 'b1': b1, 'W2': W2, 'b2': b2}
    _L0_ffn_all = _L0_ffn_setup()
    _L0_ffn_in = {k: v for k, v in _L0_ffn_all.items() if k in ('Wg', 'W1', 'b1', 'W2', 'b2')}
    del _L0_ffn_all
    return {'x': x, 'ctx_1024': ctx_1024, 'mask_BxS2_bf1': mask_BxS2_bf1, 'g_xattn': g_xattn, 'g_ffn': g_ffn, 'L0_xattn_Wq': _L0_xattn_in['Wq'], 'L0_xattn_bq': _L0_xattn_in['bq'], 'L0_xattn_Wk': _L0_xattn_in['Wk'], 'L0_xattn_bk': _L0_xattn_in['bk'], 'L0_xattn_Wv': _L0_xattn_in['Wv'], 'L0_xattn_bv': _L0_xattn_in['bv'], 'L0_xattn_Wo': _L0_xattn_in['Wo'], 'L0_xattn_bo': _L0_xattn_in['bo'], 'L0_ffn_Wg': _L0_ffn_in['Wg'], 'L0_ffn_W1': _L0_ffn_in['W1'], 'L0_ffn_b1': _L0_ffn_in['b1'], 'L0_ffn_W2': _L0_ffn_in['W2'], 'L0_ffn_b2': _L0_ffn_in['b2']}

def reference(x, ctx_1024, mask_BxS2_bf1, g_xattn, g_ffn, L0_xattn_Wq, L0_xattn_bq, L0_xattn_Wk, L0_xattn_bk, L0_xattn_Wv, L0_xattn_bv, L0_xattn_Wo, L0_xattn_bo, L0_ffn_Wg, L0_ffn_W1, L0_ffn_b1, L0_ffn_W2, L0_ffn_b2):
    import jax
    import jax.numpy as jnp

    def _L0_xattn_ref(q, k, v, kv_mask, Wq, bq, Wk, bk, Wv, bv, Wo, bo):
        import jax, jax.numpy as jnp
        import numpy as np
        D_MODEL = 256
        N_HEADS = 16
        HEAD_DIM = D_MODEL // N_HEADS
        B, Qlen, _ = q.shape
        Klen = k.shape[1]
        qh = (q @ Wq.T + bq).reshape(B, Qlen, N_HEADS, HEAD_DIM).transpose(0, 2, 1, 3)
        kh = (k @ Wk.T + bk).reshape(B, Klen, N_HEADS, HEAD_DIM).transpose(0, 2, 1, 3)
        vh = (v @ Wv.T + bv).reshape(B, Klen, N_HEADS, HEAD_DIM).transpose(0, 2, 1, 3)
        score = jnp.einsum('bhqd,bhkd->bhqk', qh, kh) / np.sqrt(HEAD_DIM).astype(np.float32)
        score = jnp.where(kv_mask[:, None, None, :], score, jnp.float32(-10000.0))
        attn = jax.nn.softmax(score, axis=-1)
        out = jnp.einsum('bhqk,bhkd->bhqd', attn, vh)
        out = out.transpose(0, 2, 1, 3).reshape(B, Qlen, D_MODEL)
        return out @ Wo.T + bo

    def _L0_ffn_ref(x, Wg, W1, b1, W2, b2):
        import jax, jax.numpy as jnp
        import numpy as np
        TOP_K = 2
        b, l, d = x.shape
        E = Wg.shape[1]
        xt = x.reshape(b * l, d)
        N = xt.shape[0]
        S = jax.nn.sigmoid(xt @ Wg)
        G, I = jax.lax.top_k(S, TOP_K)
        h = jax.nn.gelu(jnp.einsum('nd,edf->enf', xt, W1) + b1[:, None, :])
        y = jnp.einsum('enf,efd->end', h, W2) + b2[:, None, :]
        combine = jnp.zeros((N, E), dtype=x.dtype).at[jnp.arange(N)[:, None], I].add(G)
        out = jnp.einsum('ne,end->nd', combine, y)
        return out.reshape(b, l, d)
    x = x + jnp.tanh(g_xattn[0]) * _L0_xattn_ref(_layernorm(x, axis=-1), ctx_1024, ctx_1024, mask_BxS2_bf1, L0_xattn_Wq, L0_xattn_bq, L0_xattn_Wk, L0_xattn_bk, L0_xattn_Wv, L0_xattn_bv, L0_xattn_Wo, L0_xattn_bo)
    x = x + jnp.tanh(g_ffn[0]) * _L0_ffn_ref(_layernorm(x, axis=-1), L0_ffn_Wg, L0_ffn_W1, L0_ffn_b1, L0_ffn_W2, L0_ffn_b2)
    return x

_drawn_inputs = setup_inputs


def setup_inputs(seed=0):
    import zlib

    import numpy as np

    out = dict(_drawn_inputs(seed))
    spreads = {'L0_xattn_bq': (0.0, 0.1),
     'L0_xattn_bk': (0.0, 0.1),
     'L0_xattn_bv': (0.0, 0.1),
     'L0_xattn_bo': (0.0, 0.1),
     'L0_ffn_b1': (0.0, 0.1),
     'L0_ffn_b2': (0.0, 0.1)}
    factors = {}
    for name, (base, spread) in spreads.items():
        noise = np.random.default_rng([zlib.crc32(name.encode()), seed]).standard_normal(out[name].shape)
        drawn = base * np.exp(spread * noise) if base else spread * noise
        out[name] = jnp.asarray(drawn.astype(out[name].dtype))
    for name, factor in factors.items():
        out[name] = (out[name] * factor).astype(out[name].dtype)
    return out
```

```python
from contextlib import ExitStack

import concourse.bass as bass
import numpy as np
from concourse import mybir

P = 128
F32, F16, I32, U8 = mybir.dt.float32, mybir.dt.float16, mybir.dt.int32, mybir.dt.uint8
ALU = mybir.AluOpType
ACT = mybir.ActivationFunctionType
AX_X = mybir.AxisListType.X

N_HEADS = 16
TOP_K = 2
EPS = 1e-5
RSQRT_MAGIC = 0x5F3759DF
MASKED = -10000.0
TILES_PER_UNIT = 2


def build(nc, x, ctx, mask, g_xattn, g_ffn, wq, bq, wk, bk, wv, bv, wo, bo, wg, w1, b1, w2, b2, out):
    B, L, D = x.shape
    S = ctx.shape[1]
    E = wg.shape[1]
    F = w1.shape[2]
    N = B * L
    T = N // P
    HD = D // N_HEADS
    KC = D // P
    NPAIR = N_HEADS // 2
    UT = TILES_PER_UNIT * P
    U = N // UT
    UNITS_PER_BATCH = L // UT
    S2 = S - P
    SP = P + 32
    FC = F // P
    NT = (N * TOP_K + E * (P - 1)) // P
    TAB = NT + 2
    W_CHUNK = 1024
    W_SCALE = 64.0
    LOOP = (NT - 5) // 2
    assert NT % 2 == 1
    assert D == 256 and HD == 16 and 0 < S2 <= 32 and E == 8

    ROW_ONE = 96
    ROW_MAX = 97
    ROWS = ROW_MAX + N_HEADS
    SCORE_SCALE = 1.0 / float(np.sqrt(HD))
    MASK_ADDEND = MASKED / SCORE_SCALE

    x_t = x.rearrange("b l d -> (b l) d").rearrange("(t p) d -> p t d", p=P)
    out_t = out[0:N, :].rearrange("(t p) d -> p t d", p=P)
    xn2_dram = nc.dram_tensor("xn2_scratch", [N, D], F32).ap()
    xn2_t = xn2_dram.rearrange("(t p) d -> p t d", p=P)

    es = ExitStack()
    with es:
        def sb(name, shape, dt=F32):
            return es.enter_context(nc.sbuf_tensor(name, shape, dt))

        def sem(name):
            return es.enter_context(nc.semaphore(name))

        X = sb("X", [P, T, D])
        W1H, W1L = sb("W1H", [P, E * KC * F], F16), sb("W1L", [P, E * KC * F], F16)
        W2H = sb("W2H", [P, E * FC * D], F16)
        b1T = sb("b1T", [P, E * FC])
        bias_q, bias_o = sb("bias_q", [P, KC]), sb("bias_o", [P, D])
        gates, tanh_g = sb("gates", [P, 2]), sb("tanh_g", [P, 2])
        wg_sb, b2_sb = sb("wg_sb", [P, KC, E]), sb("b2_sb", [E, D])
        ident, pad_mask = sb("ident", [P, P]), sb("pad_mask", [P, 1])
        Z = sb("Z", [P, T, E])
        expert_of = sb("expert_of", [1, TAB], I32)
        gather_tab, scatter_tab = sb("gather_tab", [P, TAB], I32), sb("scatter_tab", [P, TAB], I32)
        gate_tab = sb("gate_tab", [P, TAB])

        W_stage = [sb(f"W_stage{i}", [P, W_CHUNK]) for i in range(2)]

        with ExitStack() as es_setup:
            outer, es = es, es_setup
            ctx_a, ctx_b = sb("ctx_a", [P, B, D]), sb("ctx_b", [S2, B, D])
            W_nat = sb("W_nat", [P, 4, KC, D])
            WT_kv = sb("WT_kv", [P, 2, KC, D])
            ctxT = sb("ctxT", [P, KC, B, SP])
            ctxT_late = sb("ctxT_late", [P, KC, B, 4, SP - P])
            b1_nat = sb("b1_nat", [E * FC, P])
            bias_k, bias_v, bias_v_pad = sb("bias_k", [P, KC]), sb("bias_v", [P, D]), sb("bias_v_pad", [P, D])
            stats1 = sb("stats1", [P, T, 6])
            var1, newton1, half_bits1 = sb("var1", [P, T]), sb("newton1", [P, T]), sb("half_bits1", [P, T], I32)
            mask_u8, mask_f = sb("mask_u8", [P, B * S], U8), sb("mask_f", [P, B * S])
            kf = sb("kf", [P, KC, B * S])
            kh, kl = sb("kh", [P, KC, B * S], F16), sb("kl", [P, KC, B * S], F16)
            es = outer
        W2L = sb("W2L", [P, E * FC * D], F16)

        with ExitStack() as es_attn:
            outer, es = es, es_attn
            WT_qo = sb("WT_qo", [P, 2, KC, D])
            kst = sb("kst", [P, B, NPAIR, 2, SP], F16)
            kst_late = sb("kst_late", [P, B, NPAIR, 2 * (SP - P)], F16)
            v_a = sb("v_a", [P, B, N_HEADS, HD + 1])
            v_b = sb("v_b", [P, B, 4, 4, HD + 1])
            qst = [sb(f"qst{i}", [P, NPAIR, UT], F16) for i in range(3)]
            qh, ql = sb("qh", [P, KC, UT], F16), sb("ql", [P, KC, UT], F16)
            stats, mv = sb("stats", [P, 2, 6]), sb("mv", [P, 2, 2])
            mv1, rstd1 = sb("mv1", [P, T, 2]), sb("rstd1", [P, T])
            var, rstd, newton = sb("var", [P, 2]), sb("rstd", [P, 2]), sb("newton", [P, 2])
            half_bits = sb("half_bits", [P, 2], I32)
            xn, xnT = sb("xn", [P, 2, D]), sb("xnT", [P, KC, UT])
            rowmax, negmax = sb("rowmax", [P, 2 * N_HEADS]), sb("negmax", [P, P])
            negmaxT = sb("negmaxT", [2 * N_HEADS, P], F16)
            probs = sb("probs", [P, 3, 2, UT])
            recip = sb("recip", [P, 2, N_HEADS])
            attn, attnT = sb("attn", [P, 2, D]), sb("attnT", [P, 2, KC, P])
            xn2 = sb("xn2", [P, 2, D])
            xn2T = attnT
            es = outer

        with ExitStack() as es_route:
            outer, es = es, es_route
            before = sb("before", [P, P], F16)
            ones = sb("ones", [P, P], F16)
            iota_slot, iota_tile = sb("iota_slot", [P, P]), sb("iota_tile", [P, TAB])
            token_no, spare_row = sb("token_no", [P, TOP_K * T]), sb("spare_row", [P, 1])
            lower = sb("lower", [P, E, E])
            exp_z, sig = sb("exp_z", [P, T, E]), sb("sig", [P, T, E])
            ahead, tie = sb("ahead", [P, T, E, E]), sb("tie", [P, T, E, E])
            rank = sb("rank", [P, T * E])
            chosen = sb("chosen", [P, TOP_K, T * E])
            chosen16 = sb("chosen16", [P, T * E], F16)
            combine = sb("combine", [P, T, E])
            combineT = sb("combineT", [E, T, P])
            n_int, n_tiles, tile_end, tile_base, no_add = (sb("n_int", [P, E], I32), sb("n_tiles", [P, E]), sb("tile_end", [P, E]),
                                                            sb("tile_base", [P, E]), sb("no_add", [P, E]))
            slot_e = sb("slot_e", [P, T * E])
            picked = sb("picked", [P, TOP_K, T * E])
            slot, gate = sb("slot", [P, TOP_K * T]), sb("gate", [P, TOP_K * T])
            slot_i, tile_i, place_i = (sb(n, [P, TOP_K * T], I32) for n in ("slot_i", "tile_i", "place_i"))
            tile_f, place_f = sb("tile_f", [P, TOP_K * T]), sb("place_f", [P, TOP_K * T])
            at_place = sb("at_place", [P, TOP_K * T, P])
            tab_rhs = sb("tab_rhs", [P, TOP_K * T, 2, TAB])
            empty, token_m1 = sb("empty", [P, TAB]), sb("token_m1", [P, TAB])
            past = sb("past", [1, TAB, E])
            expert_f = sb("expert_f", [1, TAB])
            es = outer
        xg = [sb(f"xg{i}", [P, D]) for i in range(2)]
        gather_col = [sb(f"gather_col{i}", [P, 1], I32) for i in range(2)]
        scatter_col = [sb(f"scatter_col{i}", [P, 1], I32) for i in range(2)]
        xh, xl = ([sb(f"{n}{i}", [P, KC * P], F16) for i in range(2)] for n in ("xh", "xl"))
        h32 = [sb(f"h32_{i}", [P, FC * P]) for i in range(2)]
        hh, hl = ([sb(f"{n}{i}", [P, FC * P], F16) for i in range(2)] for n in ("hh", "hl"))
        y_sb = [sb(f"y_sb{i}", [P, D]) for i in range(2)]

        bank = [es.enter_context(nc.psum_tensor(f"bank{i}", [P, 512], F32)) for i in range(8)]
        XT_BANKS, Y_BANKS, H_BANKS = bank[4:6], bank[6:8], (bank[0:2], bank[2:4])
        S2_BANKS, PV_BANKS, A_BANK, Q_BANK, S1_BANKS = bank[0:2], bank[2:4], bank[4], bank[5], bank[6:8]

        x_loaded = [sem(f"x_loaded{u}") for u in range(U)]
        ctx_loaded, w_loaded, bias_loaded = sem("ctx_loaded"), sem("w_loaded"), sem("bias_loaded")
        zeroed, consts_made, select_made = sem("zeroed"), sem("consts_made"), sem("select_made")
        mask_row_made, tanh_made = sem("mask_row_made"), sem("tanh_made")
        setup_filled, setup_evac_act, setup_evac_dve = sem("setup_filled"), sem("setup_evac_act"), sem("setup_evac_dve")
        kv_filled, kv_made, kst_landed, mask_made = sem("kv_filled"), sem("kv_made"), sem("kst_landed"), sem("mask_made")
        v_made, ctx_late_made, kst_late_made = sem("v_made"), sem("ctx_late_made"), sem("kst_late_made")
        bo_gated = sem("bo_gated")
        dve_step = sem("dve_step")
        ln1_done, x_biased = sem("ln1_done"), sem("x_biased")
        a_filled, a_evac, q_filled, q_high, q_free = sem("a_filled"), sem("a_evac"), sem("q_filled"), sem("q_high"), sem("q_free")
        qst_landed = [sem(f"qst_landed{i}") for i in range(3)]
        max_landed = [sem(f"max_landed{i}") for i in range(3)]
        s1_filled, rowmax_done, negmax_done = sem("s1_filled"), sem("rowmax_done"), sem("negmax_done")
        s2_filled, exp_done, pv_done, attn_normed = sem("s2_filled"), sem("exp_done"), sem("pv_done"), sem("attn_normed")
        x2_done, ln2_done = sem("x2_done"), sem("ln2_done")
        xn2_stored = sem("xn2_stored")
        consts2_made = sem("consts2_made")
        w_staged, w_used, w_ready = [sem("w_staged0"), sem("w_staged1")], sem("w_used"), sem("w_ready")
        w_high = sem("w_high")
        exp_z_made, chosen_made, comb_made = sem("exp_z_made"), sem("chosen_made"), sem("comb_made")
        ranked, combT_filled, combT_made = sem("ranked"), sem("combT_filled"), sem("combT_made")
        tab_rhs_made, tab_filled, tables_made = sem("tab_rhs_made"), sem("tab_filled"), sem("tables_made")
        init_filled, init_added, init_stored = sem("init_filled"), sem("init_added"), sem("init_stored")
        cols_made, gather_issued, scatter_issued = sem("cols_made"), sem("gather_issued"), sem("scatter_issued")
        gathered = [sem("gathered0"), sem("gathered1")]
        xt_filled, xh_made, xl_made = sem("xt_filled"), sem("xh_made"), sem("xl_made")
        h_filled, gelu_done, hh_made, hl_made = sem("h_filled"), sem("gelu_done"), sem("hh_made"), sem("hl_made")
        y_filled, y_made, scattered = sem("y_filled"), sem("y_made"), sem("scattered")

        ITEMS = NPAIR + 2
        MAX_ITEMS = 4
        FRAMES = range(-2, U + 1)

        def live(u):
            return 0 <= u < U

        A_USES = [(k, u + d) for u in FRAMES for k, d in (("xT", 2), ("attnT", -1), ("maxT", 1), ("xn2T", -1)) if live(u + d)]
        Q_USES = [(k, u + d) for u in FRAMES for k, d in (("q", 2), ("wo", -1), ("logits", -1)) if live(u + d)]
        a_nth = {use: n + 1 for n, use in enumerate(A_USES)}
        q_nth = {use: n + 1 for n, use in enumerate(Q_USES)}
        QST_PER_USE, MAX_PER_USE = 12 * 16, 2 * 16
        KST_LANDED = 16 * 8 * 3 * KC

        def item_heads(i):
            return ("pair", i if i < 4 else i - 1) if i % 5 != 4 else ("late", i // 5)

        chunks = [(w1[e, k * P:(k + 1) * P, :], W1H, W1L, (e * KC + k) * F) for e in range(E) for k in range(KC)]
        chunks += [(w2[e, k * P:(k + 4) * P, :].rearrange("(c p) d -> p c d", p=P), W2H, W2L, (e * FC + k) * D)
                   for e in range(E) for k in range(0, FC, 4)]
        W_PER_FRAME = -(-len(chunks) // len(FRAMES))
        assert W_PER_FRAME == 3

        block = es.enter_context(nc.Block())

        @block.sync
        def _(sp):
            sp.dma_start(ctx_a[:, :, :], ctx[:, 0:P, :].rearrange("b s d -> s b d")).then_inc(ctx_loaded, 16)
            sp.dma_start(ctx_b[:, :, :], ctx[:, P:S, :].rearrange("b s d -> s b d")).then_inc(ctx_loaded, 16)
            for u in range(2):
                sp.dma_start(X[:, 2 * u:2 * u + 2, :], x_t[:, 2 * u:2 * u + 2, :]).then_inc(x_loaded[u], 16)
            for n, w in enumerate((wq, wk, wv, wo)):
                sp.dma_start(W_nat[:, n, :, :], w.rearrange("(c p) d -> p c d", p=P)).then_inc(w_loaded, 16)
            for u in range(2, U):
                sp.dma_start(X[:, 2 * u:2 * u + 2, :], x_t[:, 2 * u:2 * u + 2, :]).then_inc(x_loaded[u], 16)
            sp.wait_ge(kv_made, 2 * KC)
            sp.wait_ge(zeroed, 2)
            for r in range(8):
                for grp, src in enumerate((kh, kh, kl)):
                    for c in range(KC):
                        row = 32 * grp + 16 * (r % 2)
                        sp.dma_start(kst[row:row + 16, :, 4 * c + r // 2, r % 2, 0:S],
                                     src[16 * r:16 * r + 16, c, :].rearrange("p (b s) -> p b s", b=B)).then_inc(kst_landed, 16)
            for u in FRAMES:
                if live(u + 2):
                    v = u + 2
                    if v >= 3:
                        sp.wait_ge(s2_filled, ITEMS * (v - 2))
                    sp.wait_ge(q_high, v + 1)
                    for grp in (0, 2):
                        for r in range(4):
                            sp.dma_start(qst[v % 3][32 * grp:32 * grp + 32, r:NPAIR:4, :],
                                         qh[32 * r:32 * r + 32, :, :]).then_inc(qst_landed[v % 3], 16)
                    sp.wait_ge(q_free, q_nth["q", v])
                    for r in range(4):
                        sp.dma_start(qst[v % 3][32:64, r:NPAIR:4, :],
                                     ql[32 * r:32 * r + 32, :, :]).then_inc(qst_landed[v % 3], 16)
                if live(u + 1):
                    v = u + 1
                    sp.wait_ge(a_evac, a_nth["maxT", v])
                    for j in range(2):
                        sp.dma_start(qst[v % 3][ROW_MAX:ROWS, :, j * P:(j + 1) * P],
                                     negmaxT[16 * j:16 * j + 16, :].unsqueeze(1).broadcast_to([16, NPAIR, P])
                                     ).then_inc(max_landed[v % 3], 16)
                if live(u - 1):
                    v = u - 1
                    sp.wait_ge(ln2_done, v + 1)
                    sp.dma_start(xn2_t[:, 2 * v:2 * v + 2, :], xn2[:, :, :]).then_inc(xn2_stored, 16)
            for q in range(4):
                sp.wait_ge(init_added, 2 * q + 2)
                sp.dma_start(out_t[:, 4 * q:4 * q + 4, :], X[:, 4 * q:4 * q + 4, :]).then_inc(init_stored, 16)
            sp.dma_start(out[N:N + P, :], X[:, 0, :]).then_inc(init_stored, 16)
            sp.wait_ge(init_stored, 16 * 5)

        @block.gpsimd
        def _(pool):
            nc.gpsimd.memset(kst[:, 0, :, :, :], 0.0).then_inc(zeroed, 1)
            nc.gpsimd.memset(kst[:, 1, :, :, :], 0.0).then_inc(zeroed, 1)
            nc.gpsimd.memset(ident[:, :], 0.0).then_inc(zeroed, 1)
            nc.gpsimd.memset(pad_mask[:, :], 1.0).then_inc(zeroed, 1)
            pool.wait_ge(zeroed, 4)
            nc.gpsimd.affine_select(out=ident[:, :], in_=ident[:, :], compare_op=ALU.not_equal, fill=1.0, base=0,
                                    pattern=[[-1, P]], channel_multiplier=1).then_inc(consts_made, 1)
            for j in range(4):
                pool.wait_ge(consts_made, j + 1)
                part = pad_mask[32 * j:32 * j + 32, :]
                nc.gpsimd.affine_select(out=part, in_=part, compare_op=ALU.is_ge, fill=0.0, base=S2 - 1,
                                        pattern=[[0, 1]], channel_multiplier=-1).then_inc(consts_made, 1)
            pool.wait_ge(consts_made, 5)
            for b in range(B):
                if b:
                    pool.wait_ge(select_made, b)
                sel = kst[ROW_ONE:ROW_ONE + 32, b, :, :, 0:S].rearrange("p n a s -> p (n a) s")
                nc.gpsimd.affine_select(out=sel, in_=sel, compare_op=ALU.not_equal, fill=1.0, base=-1,
                                        pattern=[[-1, N_HEADS], [0, S]], channel_multiplier=1).then_inc(select_made, 1)
            with nc.allow_non_contiguous_dma(reason="bias columns"):
                pool.dma_start(bias_q[:, :], bq.rearrange("(c p) -> p c", p=P)).then_inc(bias_loaded, 16)
                pool.dma_start(bias_k[:, :], bk.rearrange("(c p) -> p c", p=P)).then_inc(bias_loaded, 16)
            pool.dma_start(bias_v[:, :], bv.partition_broadcast(P)).then_inc(bias_loaded, 16)
            pool.dma_start(bias_o[:, :], bo.partition_broadcast(P)).then_inc(bias_loaded, 16)
            pool.dma_start(gates[:, 0:1], g_xattn.partition_broadcast(P)).then_inc(bias_loaded, 16)
            pool.dma_start(gates[:, 1:2], g_ffn.partition_broadcast(P)).then_inc(bias_loaded, 16)
            pool.dma_start(mask_u8[:, :], mask.rearrange("b s -> (b s)").partition_broadcast(P)).then_inc(bias_loaded, 16)
            pool.dma_start(wg_sb[:, :, :], wg.rearrange("(c p) e -> p c e", p=P)).then_inc(bias_loaded, 16)
            pool.dma_start(b2_sb[:, :], b2).then_inc(bias_loaded, 16)
            pool.dma_start(b1_nat[:, :], b1.rearrange("e (m p) -> (e m) p", p=P)).then_inc(bias_loaded, 16)
            def load(n):
                src = chunks[n][0]
                dst = W_stage[n % 2][:, :]
                if len(src.shape) == 3:
                    dst = dst.rearrange("p (c d) -> p c d", c=4)
                pool.dma_start(dst, src).then_inc(w_staged[n % 2], 16)

            load(0)
            load(1)
            pool.wait_ge(bo_gated, 1)
            for n, (_, high, low, at) in enumerate(chunks):
                stage = W_stage[n % 2]
                if n % W_PER_FRAME == 0 and n // W_PER_FRAME < U:
                    u = n // W_PER_FRAME
                    pool.wait_ge(ln1_done, u + 1)
                    nc.gpsimd.tensor_tensor(X[:, 2 * u:2 * u + 2, :], X[:, 2 * u:2 * u + 2, :],
                                            bias_o[:, :].unsqueeze(1).broadcast_to([P, 2, D]), ALU.add).then_inc(x_biased, 1)
                pool.wait_ge(w_high, n + 1)
                if high is W2H and at == 0:
                    pool.wait_ge(kst_late_made, 1)
                nc.gpsimd.tensor_tensor(low[:, at:at + W_CHUNK], stage[:, :], high[:, at:at + W_CHUNK], ALU.subtract).then_inc(w_ready, 1)
                if n + 2 < len(chunks):
                    pool.wait_ge(w_ready, n + 1)
                    load(n + 2)

            pool.wait_ge(q_free, len(Q_USES))
            pool.wait_ge(xn2_stored, 16 * U)
            nc.gpsimd.memset(ones[:, :], 1.0).then_inc(consts2_made, 1)
            nc.gpsimd.memset(before[:, :], 1.0).then_inc(consts2_made, 1)
            nc.gpsimd.memset(lower[:, :, :], 1.0).then_inc(consts2_made, 1)
            pool.wait_ge(consts2_made, 3)
            nc.gpsimd.affine_select(out=before[:, :], in_=before[:, :], compare_op=ALU.is_gt, fill=0.0, base=0,
                                    pattern=[[1, P]], channel_multiplier=-1).then_inc(consts2_made, 1)
            nc.gpsimd.affine_select(out=lower[:, :, :], in_=lower[:, :, :], compare_op=ALU.is_gt, fill=0.0, base=0,
                                    pattern=[[1, E], [-1, E]], channel_multiplier=0).then_inc(consts2_made, 1)
            exact = dict(allow_small_or_imprecise_dtypes=True)
            nc.gpsimd.iota(iota_slot[:, :], pattern=[[1, P]], base=0, channel_multiplier=0, **exact).then_inc(consts2_made, 1)
            nc.gpsimd.iota(iota_tile[:, :], pattern=[[1, TAB]], base=0, channel_multiplier=0, **exact).then_inc(consts2_made, 1)
            nc.gpsimd.iota(token_no[:, :], pattern=[[0, TOP_K], [P, T]], base=1, channel_multiplier=1, **exact).then_inc(consts2_made, 1)
            nc.gpsimd.iota(spare_row[:, :], pattern=[[0, 1]], base=N + 1, channel_multiplier=1, **exact).then_inc(consts2_made, 1)

            def gather(t, par):
                pool.wait_ge(cols_made, t + 1)
                pool.sem_inc(gather_issued, 1)
                nc.gpsimd.indirect_dma_start(out=xg[par][:, :], out_offset=None, in_=xn2_dram,
                                             in_offset=bass.IndirectOffsetOnAxis(ap=gather_col[par][:, 0:1], axis=0)
                                             ).then_inc(gathered[par], 16)

            def scatter(t, par, first=False):
                pool.wait_ge(y_made, t + 1)
                if not first:
                    pool.wait_ge(scattered, 16 * t)
                pool.sem_inc(scatter_issued, 1)
                nc.gpsimd.indirect_dma_start(out=out, out_offset=bass.IndirectOffsetOnAxis(ap=scatter_col[par][:, 0:1], axis=0),
                                             in_=y_sb[par][:, :], in_offset=None, compute_op=ALU.add).then_inc(scattered, 16)

            gather(0, 0)
            gather(1, 1)
            pool.wait_ge(xt_filled, 1)
            gather(2, 0)
            pool.wait_ge(init_stored, 16 * 5)
            pool.wait_ge(xt_filled, 2)
            gather(3, 1)
            scatter(0, 0, first=True)

            def two_tiles(t):
                for d in range(2):
                    pool.wait_ge(xt_filled, t + (d + 2))
                    gather(t + (d + 3), d)
                    scatter(t + d, 1 - d)

            two_tiles(1)
            with pool.Fori(0, LOOP) as pair:
                two_tiles(pair * 2 + 3)
            scatter(NT - 2, 1)
            scatter(NT - 1, 0)
            pool.wait_ge(scattered, 16 * NT)
            for par in range(2):
                pool.wait_ge(gathered[par], 16 * (NT + 1) // 2)

        BIAS_DMAS = 10

        @block.scalar
        def _(act):
            act.wait_ge(bias_loaded, 16 * BIAS_DMAS)
            nc.scalar.activation(tanh_g[:, :], gates[:, :], ACT.Tanh).then_inc(tanh_made, 1)
            act.wait_ge(select_made, 2)
            act.wait_ge(mask_made, 1)
            for b in range(B):
                nc.scalar.activation(kst[ROW_ONE:ROW_ONE + 1, b, :, :, 0:S].rearrange("p n a s -> p (n a) s"),
                                     mask_f[ROW_ONE:ROW_ONE + 1, b * S:(b + 1) * S].unsqueeze(1).broadcast_to([1, N_HEADS, S]),
                                     ACT.Copy, scale=-MASK_ADDEND, bias=MASK_ADDEND).then_inc(mask_row_made, 1)
            for n in (0, 2, 4, 6):
                act.wait_ge(setup_filled, n + 1)
                if n == 0:
                    ins = nc.scalar.activation(ctxT[:, :, 0, 0:S], bank[0][:, 0:KC * SP].rearrange("p (c s) -> p c s", c=KC)[:, :, 0:S], ACT.Copy)
                elif n == 6:
                    ins = nc.scalar.activation(b1T[:, :], bank[6][:, 0:E * FC], ACT.Copy)
                else:
                    ins = nc.scalar.activation({2: WT_kv[:, 0, :, :], 4: WT_qo[:, 0, :, :]}[n].rearrange("p c d -> p (c d)"), bank[n][:, :], ACT.Copy)
                ins.then_inc(setup_evac_act, 1)
            def weights_high(n):
                _, high, _, at = chunks[n]
                stage = W_stage[n % 2]
                act.wait_ge(w_staged[n % 2], 16 * (n // 2 + 1))
                nc.scalar.activation(high[:, at:at + W_CHUNK], stage[:, :], ACT.Copy, scale=W_SCALE)
                nc.scalar.activation(stage[:, :], stage[:, :], ACT.Copy, scale=W_SCALE).then_inc(w_high, 1)

            for u in FRAMES:
                for i in range(ITEMS):
                    if i == 0 and live(u + 2):
                        v = u + 2
                        act.wait_ge(a_filled, a_nth["xT", v])
                        if v >= 1:
                            act.wait_ge(q_filled, q_nth["q", v - 1])
                        nc.scalar.activation(xnT[:, :, :].rearrange("p c t -> p (c t)"), A_BANK[:, :], ACT.Copy).then_inc(a_evac, 1)
                    if live(u):
                        g = ITEMS * u + i
                        act.wait_ge(s2_filled, g + 1)
                        if g >= 3:
                            act.wait_ge(pv_done, g - 2)
                        nc.scalar.activation(probs[:, g % 3, :, :].rearrange("p a t -> p (a t)"), S2_BANKS[g % 2][:, :],
                                             ACT.Exp, scale=SCORE_SCALE).then_inc(exp_done, 1)
                    if i == 2 and live(u - 1):
                        v = u - 1
                        act.wait_ge(a_filled, a_nth["attnT", v])
                        if v >= 1:
                            act.wait_ge(q_filled, q_nth["wo", v - 1])
                        nc.scalar.activation(attnT[:, :, :, :].rearrange("p j c t -> p (j c t)"), A_BANK[:, :], ACT.Copy).then_inc(a_evac, 1)
                    if i == 1 and live(u + 2):
                        v = u + 2
                        act.wait_ge(q_filled, q_nth["q", v])
                        if v >= 1:
                            act.wait_ge(qst_landed[(v - 1) % 3], QST_PER_USE * ((v - 1) // 3 + 1))
                        for c in range(KC):
                            ins = nc.scalar.activation(qh[:, c, :], Q_BANK[:, c * UT:(c + 1) * UT], ACT.Identity, bias=bias_q[:, c:c + 1])
                        ins.then_inc(q_high, 1)
                    if i == 5 and live(u + 1):
                        v = u + 1
                        act.wait_ge(a_filled, a_nth["maxT", v])
                        if v >= 1:
                            act.wait_ge(max_landed[(v - 1) % 3], MAX_PER_USE * ((v - 1) // 3 + 1))
                        nc.scalar.activation(negmaxT[:, :], A_BANK[0:2 * N_HEADS, 0:P], ACT.Copy).then_inc(a_evac, 1)
                    if i in (3, 6, 8):
                        n = W_PER_FRAME * (u - FRAMES[0]) + (3, 6, 8).index(i)
                        if n < len(chunks):
                            weights_high(n)
                    if i == 7 and live(u - 1):
                        v = u - 1
                        act.wait_ge(a_filled, a_nth["xn2T", v])
                        if v >= 1:
                            act.wait_ge(q_filled, q_nth["logits", v - 1])
                        nc.scalar.activation(xn2T[:, :, :, :].rearrange("p j c t -> p (j c t)"), A_BANK[:, :], ACT.Copy).then_inc(a_evac, 1)

            act.wait_ge(q_free, len(Q_USES))
            act.wait_ge(xn2_stored, 16 * U)
            nc.scalar.activation(exp_z[:, :, :], Z[:, :, :], ACT.Exp, scale=-1.0).then_inc(exp_z_made, 1)
            for q in range(4):
                act.wait_ge(combT_filled, q + 1)
                nc.scalar.activation(combineT[:, 4 * q:4 * q + 4, :].rearrange("e t p -> e (t p)"), bank[3 + q][0:E, :], ACT.Copy).then_inc(combT_made, 1)

            def to_high(t, par):
                act.wait_ge(xt_filled, t + 1)
                nc.scalar.activation(xh[par][:, :], XT_BANKS[par][:, 0:KC * P], ACT.Copy).then_inc(xh_made, 1)

            def gelu(t, par, warm=True):
                e = act.value_load(expert_of[0:1, bass.ds(t, 1)], min_val=0, max_val=E - 1)
                if warm:
                    act.wait_ge(hl_made, 2 * t - 2)
                for half in range(2):
                    act.wait_ge(h_filled, 2 * t + half + 1)
                    for m in range(FC // 2 * half, FC // 2 * (half + 1)):
                        ins = nc.scalar.activation(h32[par][:, m * P:(m + 1) * P], H_BANKS[par][half][:, m % 4 * P:(m % 4 + 1) * P],
                                                   ACT.Gelu_apprx_tanh, scale=1.0 / W_SCALE, bias=b1T[:, bass.ds(e * FC + m, 1)])
                    ins.then_inc(gelu_done, 1)

            act.wait_ge(tables_made, 1)
            act.wait_ge(init_added, U)
            to_high(0, 0)
            to_high(1, 1)
            gelu(0, 0, warm=False)
            gelu(1, 1, warm=False)
            to_high(2, 0)

            def two_tiles(t):
                gelu(t + 1, 0)
                to_high(t + 2, 1)
                gelu(t + 2, 1)
                to_high(t + 3, 0)

            two_tiles(1)
            with act.Fori(0, LOOP) as pair:
                two_tiles(pair * 2 + 3)
            gelu(NT - 1, 0)

        @block.vector
        def _(dve):
            steps = [0]

            def step(ins):
                steps[0] += 1
                ins.then_inc(dve_step, 1)
                dve.wait_ge(dve_step, steps[0])

            for i in range(3):
                nc.vector.memset(qst[i][ROW_ONE:ROW_ONE + 1, :, :], 1.0)
            nc.vector.memset(ctxT[:, :, :, S:SP], 0.0)
            nc.vector.memset(negmax[:, :], 0.0)
            nc.vector.memset(v_a[:, :, :, :], 1.0)
            step(nc.vector.memset(v_b[:, :, :, :, :], 0.0))
            dve.wait_ge(consts_made, 5)
            for j in range(4):
                nc.vector.tensor_copy(v_b[32 * j:32 * j + 32, :, :, j, HD:HD + 1].rearrange("p b q d -> p (b q) d"),
                                      pad_mask[32 * j:32 * j + 32, :].unsqueeze(1).broadcast_to([32, 4 * B, 1]))
            dve.wait_ge(bias_loaded, 16 * BIAS_DMAS)
            nc.vector.tensor_copy(mask_f[:, :], mask_u8[:, :]).then_inc(mask_made, 1)
            nc.vector.tensor_scalar(bias_v_pad[:, :], bias_v[:, :], pad_mask[:, 0:1], None, ALU.mult)
            dve.wait_ge(tanh_made, 1)
            nc.vector.tensor_scalar(bias_o[:, :], bias_o[:, :], tanh_g[:, 0:1], None, ALU.mult).then_inc(bo_gated, 1)
            for n in (1, 3, 5):
                dve.wait_ge(setup_filled, n + 1)
                if n == 1:
                    ins = nc.vector.tensor_copy(ctxT[:, :, 1, 0:S], bank[1][:, 0:KC * SP].rearrange("p (c s) -> p c s", c=KC)[:, :, 0:S])
                else:
                    ins = nc.vector.tensor_copy({3: WT_kv[:, 1, :, :], 5: WT_qo[:, 1, :, :]}[n].rearrange("p c d -> p (c d)"), bank[n][:, :])
                ins.then_inc(setup_evac_dve, 1)
            dve.wait_ge(setup_evac_act, 1)
            dve.wait_ge(setup_evac_dve, 1)
            nc.vector.tensor_copy(ctxT_late[:, :, :, :, :].rearrange("p k b j s -> p (k b) j s"),
                                  ctxT[:, :, :, P:SP].rearrange("p k b s -> p (k b) s").unsqueeze(2).broadcast_to([P, KC * B, 4, SP - P])
                                  ).then_inc(ctx_late_made, 1)
            dve.wait_ge(mask_made, 1)
            for c in range(KC):
                dve.wait_ge(kv_filled, c + 1)
                step(nc.vector.scalar_tensor_tensor(out=kf[:, c, :], in0=bank[c][:, 0:B * S], scalar=bias_k[:, c:c + 1],
                                                    in1=mask_f[:, :], op0=ALU.add, op1=ALU.mult))
                nc.vector.tensor_copy(kh[:, c, :], kf[:, c, :]).then_inc(kv_made, 1)
                dve.wait_ge(kv_made, 2 * c + 1)
                nc.vector.tensor_tensor(kl[:, c, :], kf[:, c, :], kh[:, c, :], ALU.subtract).then_inc(kv_made, 1)
            dve.wait_ge(kv_filled, 3)
            nc.vector.tensor_tensor(v_a[:, :, :, 0:HD], bank[2][:, :].rearrange("p (b h d) -> p b h d", b=B, h=N_HEADS),
                                    bias_v[:, :].rearrange("p (h d) -> p h d", h=N_HEADS).unsqueeze(1).broadcast_to([P, B, N_HEADS, HD]),
                                    ALU.add).then_inc(v_made, 1)
            dve.wait_ge(kv_filled, 4)
            for b in range(B):
                for j in range(4):
                    rows = slice(32 * j, 32 * j + 32)
                    ins = nc.vector.scalar_tensor_tensor(
                        out=v_b[rows, b, :, j, 0:HD],
                        in0=bank[3][rows, b * D:(b + 1) * D].rearrange("p (q j d) -> p q j d", q=4, j=4)[:, :, j, :],
                        scalar=pad_mask[rows, 0:1],
                        in1=bias_v_pad[rows, :].rearrange("p (q j d) -> p q j d", q=4, j=4)[:, :, j, :],
                        op0=ALU.mult, op1=ALU.add)
            ins.then_inc(v_made, 1)

            dve.wait_ge(kst_landed, KST_LANDED)
            dve.wait_ge(mask_row_made, B)
            nc.vector.tensor_copy(kst_late[:, :, :, :].rearrange("p b n (a s) -> p (b n a) s", a=2),
                                  kst[:, :, :, :, P:SP].rearrange("p b n a s -> p (b n a) s")).then_inc(kst_late_made, 1)

            def row_stats(src, n, stats, mv, var, rstd, newton, half_bits):
                for j in range(n):
                    ins = nc.vector.bn_stats(stats[:, j, :], src[:, j, :])
                step(ins)
                for j in range(n):
                    ins = nc.vector.bn_aggr(mv[:, j, :], stats[:, j, :])
                step(ins)
                step(nc.vector.tensor_scalar(var[:, :], mv[:, :, 1], EPS, None, ALU.add))
                step(nc.vector.tensor_scalar(half_bits[:, :], var[:, :].bitcast(I32), 1, None, ALU.logical_shift_right))
                nc.vector.tensor_scalar(var[:, :], var[:, :], -0.5, None, ALU.mult)
                step(nc.vector.tensor_scalar(rstd[:, :].bitcast(I32), half_bits[:, :], -1, RSQRT_MAGIC, ALU.mult, ALU.add))
                for _ in range(3):
                    step(nc.vector.tensor_tensor(newton[:, :], rstd[:, :], rstd[:, :], ALU.mult))
                    step(nc.vector.tensor_tensor(newton[:, :], newton[:, :], var[:, :], ALU.mult))
                    step(nc.vector.scalar_tensor_tensor(out=rstd[:, :], in0=newton[:, :], scalar=1.5, in1=rstd[:, :], op0=ALU.add, op1=ALU.mult))

            def normalise(dst, src, mv, rstd):
                for j in range(2):
                    ins = nc.vector.tensor_scalar(dst[:, j, :], src[:, j, :], mv[:, j, 0:1], rstd[:, j:j + 1], ALU.subtract, ALU.mult)
                return ins

            def layernorm1(v):
                if v >= 1:
                    dve.wait_ge(a_filled, a_nth["xT", v - 1])
                normalise(xn, X[:, 2 * v:2 * v + 2, :], mv1[:, 2 * v:2 * v + 2, :], rstd1[:, 2 * v:2 * v + 2]).then_inc(ln1_done, 1)

            for u in range(U):
                dve.wait_ge(x_loaded[u], 16)
            row_stats(X, T, stats1, mv1, var1, rstd1, newton1, half_bits1)
            layernorm1(0)

            for u in FRAMES:
                for i in range(ITEMS):
                    if live(u + 1):
                        for n in range(MAX_ITEMS * i, min(MAX_ITEMS * (i + 1), 2 * NPAIR)):
                            g = 2 * NPAIR * (u + 1) + n
                            dve.wait_ge(s1_filled, g + 1)
                            nc.vector.reduce_max(rowmax[:, 2 * n:2 * n + 2],
                                                 S1_BANKS[g % 2][:, 0:2 * S].rearrange("p (a s) -> p a s", a=2),
                                                 AX_X).then_inc(rowmax_done, 1)
                    if i == 1 and live(u - 1):
                        v = u - 1
                        dve.wait_ge(pv_done, ITEMS * (v + 1))
                        if v >= 1:
                            dve.wait_ge(a_filled, a_nth["attnT", v - 1])
                        pv = [PV_BANKS[j][:, 0:N_HEADS * (HD + 1)].rearrange("p (h d) -> p h d", h=N_HEADS) for j in range(2)]
                        for j in range(2):
                            ins = nc.vector.reciprocal(recip[:, j, :].unsqueeze(2), pv[j][:, :, HD:HD + 1])
                        step(ins)
                        for j in range(2):
                            nc.vector.tensor_tensor(attn[:, j, :].rearrange("p (h d) -> p h d", h=N_HEADS), pv[j][:, :, 0:HD],
                                                    recip[:, j, :].unsqueeze(2).broadcast_to([P, N_HEADS, HD]),
                                                    ALU.mult).then_inc(attn_normed, 1)
                    if i == 2 and live(u + 2):
                        v = u + 2
                        dve.wait_ge(q_high, v + 1)
                        if v >= 1:
                            dve.wait_ge(qst_landed[(v - 1) % 3], QST_PER_USE * ((v - 1) // 3 + 1))
                        for c in range(KC):
                            ins = nc.vector.scalar_tensor_tensor(out=ql[:, c, :], in0=Q_BANK[:, c * UT:(c + 1) * UT], scalar=bias_q[:, c:c + 1],
                                                                 in1=qh[:, c, :], op0=ALU.add, op1=ALU.subtract)
                        ins.then_inc(q_free, 1)
                    if i == 3 and live(u - 1):
                        v = u - 1
                        dve.wait_ge(q_filled, q_nth["wo", v])
                        dve.wait_ge(x_biased, v + 1)
                        unit = X[:, 2 * v:2 * v + 2, :].rearrange("p j d -> p (j d)")
                        nc.vector.scalar_tensor_tensor(out=unit, in0=Q_BANK[:, :], scalar=tanh_g[:, 0:1], in1=unit,
                                                       op0=ALU.mult, op1=ALU.add).then_inc(q_free, 1)
                    if i == 4 and live(u + 1):
                        v = u + 1
                        dve.wait_ge(rowmax_done, 2 * NPAIR * (v + 1))
                        if v >= 1:
                            dve.wait_ge(a_filled, a_nth["maxT", v - 1])
                        nc.vector.tensor_scalar(negmax[:, 0:2 * N_HEADS], rowmax[:, :], -1.0, None, ALU.mult).then_inc(negmax_done, 1)
                    if i == 4 and live(u - 1):
                        v = u - 1
                        dve.wait_ge(q_free, q_nth["wo", v])
                        if v >= 1:
                            dve.wait_ge(xn2_stored, 16 * v)
                            dve.wait_ge(a_filled, a_nth["xn2T", v - 1])
                        unit = X[:, 2 * v:2 * v + 2, :]
                        row_stats(unit, 2, stats, mv, var, rstd, newton, half_bits)
                        normalise(xn2, unit, mv, rstd).then_inc(ln2_done, 1)
                    if i == 7 and live(u + 3):
                        layernorm1(u + 3)
                    if i == 9 and live(u - 1):
                        v = u - 1
                        dve.wait_ge(q_filled, q_nth["logits", v])
                        nc.vector.tensor_copy(Z[:, 2 * v:2 * v + 2, :].rearrange("p j e -> p (j e)"), Q_BANK[:, 0:2 * E]).then_inc(q_free, 1)
            dve.wait_ge(exp_z_made, 1)
            step(nc.vector.tensor_scalar(exp_z[:, :, :], exp_z[:, :, :], 1.0, None, ALU.add))
            step(nc.vector.reciprocal(sig[:, :, :], exp_z[:, :, :]))
            mine = sig[:, :, :].unsqueeze(3).broadcast_to([P, T, E, E])
            other = sig[:, :, :].unsqueeze(2).broadcast_to([P, T, E, E])
            nc.vector.tensor_tensor(ahead[:, :, :, :], other, mine, ALU.is_gt)
            step(nc.vector.tensor_tensor(tie[:, :, :, :], other, mine, ALU.is_equal))
            dve.wait_ge(consts2_made, 9)
            flat = "p t a b -> p t (a b)"
            step(nc.vector.tensor_tensor(tie[:, :, :, :].rearrange(flat), tie[:, :, :, :].rearrange(flat),
                                         lower[:, :, :].rearrange("p a b -> p (a b)").unsqueeze(1).broadcast_to([P, T, E * E]), ALU.mult))
            step(nc.vector.tensor_tensor(ahead[:, :, :, :].rearrange(flat), ahead[:, :, :, :].rearrange(flat), tie[:, :, :, :].rearrange(flat), ALU.add))
            step(nc.vector.reduce_sum(rank[:, :], ahead[:, :, :, :].rearrange("p t a b -> p (t a) b"), AX_X))
            nc.vector.tensor_scalar(chosen16[:, :], rank[:, :], float(TOP_K), None, ALU.is_lt).then_inc(chosen_made, 1)
            for k in range(TOP_K):
                nc.vector.tensor_scalar(chosen[:, k, :], rank[:, :], float(k), None, ALU.is_equal)
            dve.wait_ge(chosen_made, 1)
            nc.vector.tensor_tensor(combine[:, :, :].rearrange("p t e -> p (t e)"), sig[:, :, :].rearrange("p t e -> p (t e)"),
                                    chosen16[:, :], ALU.mult).then_inc(comb_made, 1)
            dve.wait_ge(ranked, 2)
            nc.vector.memset(no_add[:, :], 0.0)
            step(nc.vector.tensor_scalar(n_int[:, :], bank[1][:, 0:E], float(P - 1), None, ALU.add))
            step(nc.vector.tensor_scalar(n_int[:, :], n_int[:, :], 7, None, ALU.logical_shift_right))
            step(nc.vector.tensor_copy(n_tiles[:, :], n_int[:, :]))
            step(nc.vector.tensor_tensor_scan(out=tile_end[:, :], data0=n_tiles[:, :], data1=no_add[:, :], initial=0.0, op0=ALU.add, op1=ALU.add))
            step(nc.vector.tensor_tensor(tile_base[:, :], tile_end[:, :], n_tiles[:, :], ALU.subtract))
            step(nc.vector.tensor_scalar(tile_base[:, :], tile_base[:, :], float(P), None, ALU.mult))
            step(nc.vector.tensor_tensor(slot_e[:, :].rearrange("p (t e) -> p t e", e=E), bank[0][:, 0:T * E].rearrange("p (t e) -> p t e", e=E),
                                         tile_base[:, :].unsqueeze(1).broadcast_to([P, T, E]), ALU.add))
            for src, dst in ((slot_e[:, :], slot), (sig[:, :, :].rearrange("p t e -> p (t e)"), gate)):
                step(nc.vector.tensor_tensor(picked[:, :, :], chosen[:, :, :], src.unsqueeze(1).broadcast_to([P, TOP_K, T * E]), ALU.mult))
                step(nc.vector.reduce_sum(dst[:, :], picked[:, :, :].rearrange("p k (t e) -> p (k t) e", e=E), AX_X))
            step(nc.vector.tensor_copy(slot_i[:, :], slot[:, :]))
            nc.vector.tensor_scalar(tile_i[:, :], slot_i[:, :], 7, None, ALU.logical_shift_right)
            step(nc.vector.tensor_scalar(place_i[:, :], slot_i[:, :], P - 1, None, ALU.bitwise_and))
            nc.vector.tensor_copy(tile_f[:, :], tile_i[:, :])
            step(nc.vector.tensor_copy(place_f[:, :], place_i[:, :]))
            M = TOP_K * T
            nc.vector.tensor_tensor(at_place[:, :, :], place_f[:, :].unsqueeze(2).broadcast_to([P, M, P]),
                                    iota_slot[:, :].unsqueeze(1).broadcast_to([P, M, P]), ALU.is_equal)
            step(nc.vector.tensor_tensor(tab_rhs[:, :, 0, :], tile_f[:, :].unsqueeze(2).broadcast_to([P, M, TAB]),
                                         iota_tile[:, :].unsqueeze(1).broadcast_to([P, M, TAB]), ALU.is_equal))
            for n, val in ((1, gate), (0, token_no)):
                ins = nc.vector.tensor_tensor(tab_rhs[:, :, n, :], tab_rhs[:, :, 0, :], val[:, :].unsqueeze(2).broadcast_to([P, M, TAB]), ALU.mult)
            ins.then_inc(tab_rhs_made, 1)
            step(nc.vector.tensor_tensor(past[:, :, :], iota_tile[0:1, :].unsqueeze(2).broadcast_to([1, TAB, E]),
                                    tile_end[0:1, :].unsqueeze(1).broadcast_to([1, TAB, E]), ALU.is_ge))
            step(nc.vector.reduce_sum(expert_f[:, :], past[:, :, :], AX_X))
            nc.vector.tensor_scalar(expert_of[:, :], expert_f[:, :], float(E - 1), None, ALU.min)
            dve.wait_ge(tab_filled, 1)
            nc.vector.tensor_scalar(empty[:, :], bank[2][:, 0:TAB], 0.0, None, ALU.is_equal)
            nc.vector.tensor_scalar(token_m1[:, :], bank[2][:, 0:TAB], -1.0, None, ALU.add)
            nc.vector.tensor_scalar(gather_tab[:, :], bank[2][:, 0:TAB], -1.0, 0.0, ALU.add, ALU.max)
            step(nc.vector.tensor_scalar(gate_tab[:, :], bank[2][:, TAB:2 * TAB], tanh_g[:, 1:2], 1.0 / W_SCALE, ALU.mult, ALU.mult))
            nc.vector.scalar_tensor_tensor(out=scatter_tab[:, :], in0=empty[:, :], scalar=spare_row[:, 0:1], in1=token_m1[:, :],
                                           op0=ALU.mult, op1=ALU.add).then_inc(tables_made, 1)
            for u in range(U):
                dve.wait_ge(init_filled, u + 1)
                unit = X[:, 2 * u:2 * u + 2, :].rearrange("p j d -> p (j d)")
                nc.vector.scalar_tensor_tensor(out=unit, in0=bank[3 + u % 4][:, :], scalar=tanh_g[:, 1:2], in1=unit,
                                               op0=ALU.mult, op1=ALU.add).then_inc(init_added, 1)

            def cols(t, par, warm=True):
                if warm:
                    dve.wait_ge(scattered, 16 * (t - 1))
                nc.vector.tensor_copy(scatter_col[par][:, :], scatter_tab[:, bass.ds(t, 1)])

            def gather_cols(t, par, wait):
                if wait is not None:
                    dve.wait_ge(gathered[par], wait)
                nc.vector.tensor_copy(gather_col[par][:, :], gather_tab[:, bass.ds(t, 1)]).then_inc(cols_made, 1)

            def to_low(t, par):
                dve.wait_ge(xh_made, t + 1)
                nc.vector.tensor_tensor(xl[par][:, :], XT_BANKS[par][:, 0:KC * P], xh[par][:, :], ALU.subtract).then_inc(xl_made, 1)

            def split_h(t, par, warm=True):
                for half in range(2):
                    cut = slice(FC // 2 * P * half, FC // 2 * P * (half + 1))
                    dve.wait_ge(gelu_done, 2 * t + half + 1)
                    if warm and half == 0:
                        dve.wait_ge(y_filled, t - 1)
                    nc.vector.tensor_copy(hh[par][:, cut], h32[par][:, cut]).then_inc(hh_made, 1)
                    dve.wait_ge(hh_made, 2 * t + half + 1)
                    nc.vector.tensor_tensor(hl[par][:, cut], h32[par][:, cut], hh[par][:, cut], ALU.subtract).then_inc(hl_made, 1)

            def weigh_y(t, par, warm=True):
                dve.wait_ge(y_filled, t + 1)
                cols(t, par, warm)
                nc.vector.tensor_scalar(y_sb[par][:, :], Y_BANKS[par][:, 0:D], gate_tab[:, bass.ds(t, 1)], None, ALU.mult).then_inc(y_made, 1)

            dve.wait_ge(tables_made, 1)
            gather_cols(0, 0, None)
            gather_cols(1, 1, None)
            gather_cols(2, 0, 16)
            to_low(0, 0)
            to_low(1, 1)
            gather_cols(3, 1, 16)
            split_h(0, 0, warm=False)
            split_h(1, 1, warm=False)
            to_low(2, 0)
            gather_cols(4, 0, 32)
            weigh_y(0, 0, warm=False)

            def two_tiles(t, first=False):
                split_h(t + 1, 0)
                to_low(t + 2, 1)
                gather_cols(t + 4, 1, 8 * (t + 1) + 16)
                weigh_y(t, 1, warm=not first)
                split_h(t + 2, 1)
                to_low(t + 3, 0)
                gather_cols(t + 5, 0, 8 * (t + 1) + 32)
                weigh_y(t + 1, 0)

            two_tiles(1, first=True)
            with dve.Fori(0, LOOP) as pair:
                two_tiles(pair * 2 + 3)
            split_h(NT - 1, 0)
            weigh_y(NT - 2, 1)
            weigh_y(NT - 1, 0)

        @block.tensor
        def _(pe):
            pe.wait_ge(consts_made, 1)
            pe.wait_ge(ctx_loaded, 32)
            for b in range(B):
                for c in range(KC):
                    nc.tensor.transpose(bank[b][:, c * SP:c * SP + P], ctx_a[:, b, c * P:(c + 1) * P], ident[:, :])
                    ins = nc.tensor.transpose(bank[b][:, c * SP + P:c * SP + S], ctx_b[:, b, c * P:(c + 1) * P], ident[0:S2, 0:S2])
                ins.then_inc(setup_filled, 1)
            pe.wait_ge(w_loaded, 64)
            for n, which in ((2, 1), (3, 2), (4, 0), (5, 3)):
                for c in range(KC):
                    for o in range(KC):
                        ins = nc.tensor.transpose(bank[n][:, c * D + o * P:c * D + (o + 1) * P], W_nat[:, which, o, c * P:(c + 1) * P], ident[:, :])
                ins.then_inc(setup_filled, 1)
            pe.wait_ge(bias_loaded, 16 * BIAS_DMAS)
            nc.tensor.transpose(bank[6][:, 0:E * FC], b1_nat[:, :], ident[0:E * FC, 0:E * FC]).then_inc(setup_filled, 1)
            pe.wait_ge(setup_evac_act, 4)
            pe.wait_ge(setup_evac_dve, 3)
            for c in range(KC):
                for k in range(KC):
                    ins = nc.tensor.matmul(bank[c][:, 0:B * S].rearrange("p (b s) -> p b s", b=B), WT_kv[:, 0, k, c * P:(c + 1) * P], ctxT[:, k, :, 0:S],
                                           start=(k == 0), stop=(k == KC - 1))
                ins.then_inc(kv_filled, 1)
            for b in range(B):
                for k in range(KC):
                    ins = nc.tensor.matmul(bank[2][:, b * D:(b + 1) * D], ctxT[:, k, b, 0:P], WT_kv[:, 1, k, :], start=(k == 0), stop=(k == KC - 1))
            ins.then_inc(kv_filled, 1)
            pe.wait_ge(ctx_late_made, 1)
            for b in range(B):
                for k in range(KC):
                    ins = nc.tensor.matmul(bank[3][:, b * D:(b + 1) * D], ctxT_late[:, k, b, :, :].rearrange("p j s -> p (j s)"),
                                           WT_kv[:, 1, k, :], start=(k == 0), stop=(k == KC - 1))
            ins.then_inc(kv_filled, 1)

            def a_use(kind, v):
                n = a_nth[kind, v]
                if n >= 2:
                    pe.wait_ge(a_evac, n - 1)

            def q_use(kind, v):
                n = q_nth[kind, v]
                if n >= 2:
                    pe.wait_ge(q_free, n - 1)

            def softmax_v(g):
                u, i = divmod(g, ITEMS)
                kind, n = item_heads(i)
                b = u // UNITS_PER_BATCH
                pe.wait_ge(exp_done, g + 1)
                if i == 0:
                    if u >= 1:
                        pe.wait_ge(attn_normed, 2 * u)
                    else:
                        pe.wait_ge(v_made, 2)
                for j in range(2):
                    for a in range(2):
                        lhs = probs[:, g % 3, a, j * P:(j + 1) * P]
                        if kind == "pair":
                            h = 2 * n + a
                            dst, rhs = PV_BANKS[j][:, h * (HD + 1):(h + 1) * (HD + 1)], v_a[:, b, h, :]
                        else:
                            q = 2 * n + a
                            dst, rhs = PV_BANKS[j][:, 4 * q * (HD + 1):4 * (q + 1) * (HD + 1)], v_b[:, b, q, :, :].rearrange("p j d -> p (j d)")
                        ins = nc.tensor.matmul(dst, lhs, rhs, start=(i == 0 and a == 0), stop=(kind == "late"), skip_group_check=True)
                ins.then_inc(pv_done, 1)

            for u in FRAMES:
                for i in range(ITEMS):
                    if i == 0 and live(u + 2):
                        v = u + 2
                        a_use("xT", v)
                        pe.wait_ge(ln1_done, v + 1)
                        for c in range(KC):
                            for j in range(2):
                                ins = nc.tensor.transpose(A_BANK[:, c * UT + j * P:c * UT + (j + 1) * P], xn[:, j, c * P:(c + 1) * P], ident[:, :])
                        ins.then_inc(a_filled, 1)
                    if i == 1 and live(u + 2):
                        v = u + 2
                        q_use("q", v)
                        pe.wait_ge(a_evac, a_nth["xT", v])
                        for c in range(KC):
                            for k in range(KC):
                                ins = nc.tensor.matmul(Q_BANK[:, c * UT:(c + 1) * UT], WT_qo[:, 0, k, c * P:(c + 1) * P], xnT[:, k, :], start=(k == 0), stop=(k == KC - 1))
                        ins.then_inc(q_filled, 1)
                    if live(u):
                        g = ITEMS * u + i
                        b = u // UNITS_PER_BATCH
                        kind, n = item_heads(i)
                        if g >= 2:
                            pe.wait_ge(exp_done, g - 1)
                        if i == 0:
                            pe.wait_ge(max_landed[u % 3], MAX_PER_USE * (u // 3 + 1))
                        if g == 4:
                            pe.wait_ge(kst_late_made, 1)
                        dst = S2_BANKS[g % 2]
                        if kind == "pair":
                            for a in range(2):
                                ins = nc.tensor.matmul(dst[:, a * UT:(a + 1) * UT], kst[0:ROWS, b, n, a, 0:P], qst[u % 3][0:ROWS, n, :],
                                                       start=True, stop=True)
                        else:
                            for p in range(4 * n, 4 * n + 4):
                                half, q = p % 2, (p // 2) % 2
                                ins = nc.tensor.matmul(dst[64 * half:64 * half + 64, q * UT:(q + 1) * UT], kst_late[0:ROWS, b, p, :],
                                                       qst[u % 3][0:ROWS, p, :], start=True, stop=True)
                        ins.then_inc(s2_filled, 1)
                    if live(u + 1):
                        v = u + 1
                        b = v // UNITS_PER_BATCH
                        for n in range(MAX_ITEMS * i, min(MAX_ITEMS * (i + 1), 2 * NPAIR)):
                            g = 2 * NPAIR * v + n
                            j, p = divmod(n, NPAIR)
                            if n == 0:
                                pe.wait_ge(qst_landed[v % 3], QST_PER_USE * (v // 3 + 1))
                                if v == 0:
                                    pe.wait_ge(kst_landed, KST_LANDED)
                                    pe.wait_ge(mask_row_made, B)
                            if g >= 2:
                                pe.wait_ge(rowmax_done, g - 1)
                            nc.tensor.matmul(S1_BANKS[g % 2][:, 0:2 * S].rearrange("p (a s) -> p a s", a=2), qst[v % 3][0:ROW_MAX, p, j * P:(j + 1) * P],
                                             kst[0:ROW_MAX, b, p, :, 0:S], start=True, stop=True).then_inc(s1_filled, 1)
                    if i == 0 and live(u - 1):
                        softmax_v(ITEMS * u - 1)
                    elif i >= 1 and live(u):
                        softmax_v(ITEMS * u + i - 1)
                    if i == 2 and live(u - 1):
                        v = u - 1
                        a_use("attnT", v)
                        pe.wait_ge(attn_normed, 2 * (v + 1))
                        for j in range(2):
                            for c in range(KC):
                                ins = nc.tensor.transpose(A_BANK[:, (j * KC + c) * P:(j * KC + c + 1) * P], attn[:, j, c * P:(c + 1) * P], ident[:, :])
                        ins.then_inc(a_filled, 1)
                    if i == 3 and live(u - 1):
                        v = u - 1
                        q_use("wo", v)
                        pe.wait_ge(a_evac, a_nth["attnT", v])
                        for j in range(2):
                            for c in range(KC):
                                ins = nc.tensor.matmul(Q_BANK[:, j * D:(j + 1) * D], attnT[:, j, c, :], WT_qo[:, 1, c, :], start=(c == 0), stop=(c == KC - 1))
                        ins.then_inc(q_filled, 1)
                    if i == 5 and live(u + 1):
                        v = u + 1
                        a_use("maxT", v)
                        pe.wait_ge(negmax_done, v + 1)
                        nc.tensor.transpose(A_BANK[:, 0:P], negmax[:, :], ident[:, :]).then_inc(a_filled, 1)
                    if i == 7 and live(u - 1):
                        v = u - 1
                        a_use("xn2T", v)
                        pe.wait_ge(ln2_done, v + 1)
                        for j in range(2):
                            for c in range(KC):
                                ins = nc.tensor.transpose(A_BANK[:, (j * KC + c) * P:(j * KC + c + 1) * P], xn2[:, j, c * P:(c + 1) * P], ident[:, :])
                        ins.then_inc(a_filled, 1)
                    if i == 8 and live(u - 1):
                        v = u - 1
                        q_use("logits", v)
                        pe.wait_ge(a_evac, a_nth["xn2T", v])
                        for j in range(2):
                            for c in range(KC):
                                ins = nc.tensor.matmul(Q_BANK[:, j * E:(j + 1) * E], xn2T[:, j, c, :], wg_sb[:, c, :], start=(c == 0), stop=(c == KC - 1))
                        ins.then_inc(q_filled, 1)

            pe.wait_ge(consts2_made, 5)
            pe.wait_ge(chosen_made, 1)
            nc.tensor.matmul(bank[0][:, 0:T * E], before[:, :], chosen16[:, :], start=True, stop=False, skip_group_check=True)
            for k in range(1, T):
                ins = nc.tensor.matmul(bank[0][:, k * E:T * E], ones[:, :], chosen16[:, 0:(T - k) * E], start=False, stop=(k == T - 1), skip_group_check=True)
            ins.then_inc(ranked, 1)
            for t in range(T):
                ins = nc.tensor.matmul(bank[1][:, 0:E], ones[:, :], chosen16[:, t * E:(t + 1) * E], start=(t == 0), stop=(t == T - 1))
            ins.then_inc(ranked, 1)
            pe.wait_ge(comb_made, 1)
            for t in range(T):
                ins = nc.tensor.transpose(bank[3 + t // 4][0:E, t % 4 * P:(t % 4 + 1) * P], combine[:, t, :], ident[:, :])
                if t % 4 == 3:
                    ins.then_inc(combT_filled, 1)
            pe.wait_ge(tab_rhs_made, 1)
            for n in range(TOP_K * T):
                ins = nc.tensor.matmul(bank[2][:, 0:2 * TAB], at_place[:, n, :], tab_rhs[:, n, :, :].rearrange("p v t -> p (v t)"),
                                       start=(n == 0), stop=(n == TOP_K * T - 1))
            ins.then_inc(tab_filled, 1)
            for u in range(U):
                if u < 4:
                    pe.wait_ge(combT_made, 4)
                else:
                    pe.wait_ge(init_added, u - 3)
                for j in range(2):
                    ins = nc.tensor.matmul(bank[3 + u % 4][:, j * D:(j + 1) * D], combineT[:, 2 * u + j, :], b2_sb[:, :], start=True, stop=True)
                ins.then_inc(init_filled, 1)

            def turn(t, par, nth, warm=True):
                pe.wait_ge(gathered[par], nth)
                if warm:
                    pe.wait_ge(xl_made, t - 1)
                for c in range(KC):
                    ins = nc.tensor.transpose(XT_BANKS[par][:, c * P:(c + 1) * P], xg[par][:, c * P:(c + 1) * P], ident[:, :])
                ins.then_inc(xt_filled, 1)

            def layer1(t, par, warm=True):
                e = pe.value_load(expert_of[0:1, bass.ds(t, 1)], min_val=0, max_val=E - 1)
                base = e * (KC * F)
                pe.wait_ge(xl_made, t + 1)
                for half in range(2):
                    if warm:
                        pe.wait_ge(gelu_done, 2 * t + half - 3)
                    for m in range(FC // 2 * half, FC // 2 * (half + 1)):
                        dst = H_BANKS[par][half][:, m % 4 * P:(m % 4 + 1) * P]
                        for c in range(KC):
                            cut = slice(c * P, (c + 1) * P)
                            wh = W1H[:, bass.ds(base + (c * F + m * P), P)]
                            wl = W1L[:, bass.ds(base + (c * F + m * P), P)]
                            nc.tensor.matmul(dst, wh, xh[par][:, cut], start=(c == 0), stop=False)
                            nc.tensor.matmul(dst, wh, xl[par][:, cut], start=False, stop=False)
                            ins = nc.tensor.matmul(dst, wl, xh[par][:, cut], start=False, stop=(c == KC - 1))
                    ins.then_inc(h_filled, 1)

            def layer2(t, par, warm=True):
                e = pe.value_load(expert_of[0:1, bass.ds(t, 1)], min_val=0, max_val=E - 1)
                base = e * (FC * D)
                if warm:
                    pe.wait_ge(y_made, t - 1)
                dst = Y_BANKS[par][:, 0:D]
                for m in range(FC):
                    if m % 4 == 0:
                        pe.wait_ge(hl_made, 2 * t + m // 4 + 1)
                    cut = slice(m * P, (m + 1) * P)
                    wh = W2H[:, bass.ds(base + m * D, D)]
                    wl = W2L[:, bass.ds(base + m * D, D)]
                    nc.tensor.matmul(dst, hh[par][:, cut], wh, start=(m == 0), stop=False)
                    nc.tensor.matmul(dst, hh[par][:, cut], wl, start=False, stop=False)
                    ins = nc.tensor.matmul(dst, hl[par][:, cut], wh, start=False, stop=(m == FC - 1))
                ins.then_inc(y_filled, 1)

            pe.wait_ge(tables_made, 1)
            pe.wait_ge(init_added, U)
            pe.wait_ge(w_ready, 2 * E * KC)
            turn(0, 0, 16, warm=False)
            turn(1, 1, 16, warm=False)
            layer1(0, 0, warm=False)
            layer1(1, 1, warm=False)
            turn(2, 0, 32)
            layer2(0, 0, warm=False)

            def two_tiles(t, first=False):
                layer1(t + 1, 0)
                turn(t + 2, 1, 8 * (t + 1) + 16)
                layer2(t, 1, warm=not first)
                layer1(t + 2, 1)
                turn(t + 3, 0, 8 * (t + 1) + 32)
                layer2(t + 1, 0)

            two_tiles(1, first=True)
            with pe.Fori(0, LOOP) as pair:
                two_tiles(pair * 2 + 3)
            layer1(NT - 1, 0)
            layer2(NT - 2, 1)
            layer2(NT - 1, 0)


_INS = ["x", "ctx_1024", "mask_BxS2_bf1", "g_xattn", "g_ffn", "L0_xattn_Wq", "L0_xattn_bq", "L0_xattn_Wk", "L0_xattn_bk",
        "L0_xattn_Wv", "L0_xattn_bv", "L0_xattn_Wo", "L0_xattn_bo", "L0_ffn_Wg", "L0_ffn_W1", "L0_ffn_b1", "L0_ffn_W2", "L0_ffn_b2"]


def kernel(**inputs):
    import numpy as _np
    import concourse.bacc as _bacc
    from concourse import mybir as _mybir
    from concourse.bass_utils import run_bass_kernel_spmd as _run

    nc = _bacc.Bacc("TRN2", target_bir_lowering=False, num_devices=1)
    arrays, args = {}, []
    for name in _INS:
        a = _np.ascontiguousarray(inputs[name])
        if a.dtype == _np.bool_:
            a = a.view(_np.uint8)
        arrays[f"in_{name}"] = a
        args.append(nc.dram_tensor(f"in_{name}", a.shape, _mybir.dt.from_np(a.dtype), kind="ExternalInput").ap())
    B, L, D = inputs["x"].shape
    args.append(nc.dram_tensor("out_rows", (B * L + P, D), _mybir.dt.float32, kind="ExternalOutput").ap())
    build(nc, *args)
    r = _run(nc, [arrays], core_ids=[0])
    return r.results[0]["out_rows"][0:B * L].reshape(B, L, D)
```

```python
from contextlib import ExitStack

import concourse.bass as bass
import numpy as np
from concourse import mybir

P = 128
F32, F16, I32, U8 = mybir.dt.float32, mybir.dt.float16, mybir.dt.int32, mybir.dt.uint8
ALU = mybir.AluOpType
ACT = mybir.ActivationFunctionType
AX_X = mybir.AxisListType.X

N_HEADS = 16
TOP_K = 2
EPS = 1e-5
RSQRT_MAGIC = 0x5F3759DF
MASKED = -10000.0
TILES_PER_UNIT = 2


def build(nc, x, ctx, mask, g_xattn, g_ffn, wq, bq, wk, bk, wv, bv, wo, bo, wg, w1, b1, w2, b2, out):
    B, L, D = x.shape
    S = ctx.shape[1]
    E = wg.shape[1]
    F = w1.shape[2]
    N = B * L
    T = N // P
    HD = D // N_HEADS
    KC = D // P
    NPAIR = N_HEADS // 2
    UT = TILES_PER_UNIT * P
    U = N // UT
    UNITS_PER_BATCH = L // UT
    S2 = S - P
    SP = P + 32
    FC = F // P
    NT = (N * TOP_K + E * (P - 1)) // P
    TAB = NT + 2
    W_CHUNK = 1024
    W_SCALE = 64.0
    PLACES = 8
    LOOP = (NT - 5) // 2
    assert NT % 2 == 1
    assert D == 256 and HD == 16 and 0 < S2 <= 32 and E == 8

    ROW_ONE = 96
    ROW_MAX = 97
    ROWS = ROW_MAX + N_HEADS
    SCORE_SCALE = 1.0 / float(np.sqrt(HD))
    MASK_ADDEND = MASKED / SCORE_SCALE

    x_t = x.rearrange("b l d -> (b l) d").rearrange("(t p) d -> p t d", p=P)
    out_t = out[0:N, :].rearrange("(t p) d -> p t d", p=P)
    xn2_dram = nc.dram_tensor("xn2_scratch", [N, D], F32).ap()
    xn2_t = xn2_dram.rearrange("(t p) d -> p t d", p=P)

    es = ExitStack()
    with es:
        def sb(name, shape, dt=F32):
            return es.enter_context(nc.sbuf_tensor(name, shape, dt))

        def sem(name):
            return es.enter_context(nc.semaphore(name))

        X = sb("X", [P, T, D])
        W1H, W1L = sb("W1H", [P, E * KC * F], F16), sb("W1L", [P, E * KC * F], F16)
        b1T = sb("b1T", [P, E * FC])
        bias_q, bias_o = sb("bias_q", [P, KC]), sb("bias_o", [P, D])
        gates, tanh_g = sb("gates", [P, 2]), sb("tanh_g", [P, 2])
        wg_sb, b2_sb = sb("wg_sb", [P, KC, E]), sb("b2_sb", [E, D])
        ident, pad_mask = sb("ident", [P, P]), sb("pad_mask", [P, 1])
        Z = sb("Z", [P, T, E])
        weight_col, bias_col = sb("weight_col", [1, TAB], I32), sb("bias_col", [1, TAB], I32)
        gather_tab, scatter_tab = sb("gather_tab", [P, TAB], I32), sb("scatter_tab", [P, TAB], I32)
        gate_tab = sb("gate_tab", [P, TAB])

        W_stage = [sb(f"W_stage{i}", [P, W_CHUNK]) for i in range(2)]

        with ExitStack() as es_setup:
            outer, es = es, es_setup
            sb("W2_high_place", [P, E * FC * D], F16)
            ctx_a, ctx_b = sb("ctx_a", [P, B, D]), sb("ctx_b", [S2, B, D])
            W_nat = sb("W_nat", [P, 4, KC, D])
            WT_kv = sb("WT_kv", [P, 2, KC, D])
            ctxT = sb("ctxT", [P, KC, B, SP])
            ctxT_late = sb("ctxT_late", [P, KC, B, 4, SP - P])
            b1_nat = sb("b1_nat", [E * FC, P])
            bias_k, bias_v, bias_v_pad = sb("bias_k", [P, KC]), sb("bias_v", [P, D]), sb("bias_v_pad", [P, D])
            stats1 = sb("stats1", [P, T, 6])
            var1, newton1, half_bits1 = sb("var1", [P, T]), sb("newton1", [P, T]), sb("half_bits1", [P, T], I32)
            mask_u8, mask_f = sb("mask_u8", [P, B * S], U8), sb("mask_f", [P, B * S])
            kf = sb("kf", [P, KC, B * S])
            kh, kl = sb("kh", [P, KC, B * S], F16), sb("kl", [P, KC, B * S], F16)
            es = outer
        W2 = sb("W2", [P, 2, E * FC * D], F16)

        with ExitStack() as es_attn:
            outer, es = es, es_attn
            WT_qo = sb("WT_qo", [P, 2, KC, D])
            kst = sb("kst", [P, B, NPAIR, 2, SP], F16)
            kst_late = sb("kst_late", [P, B, NPAIR, 2 * (SP - P)], F16)
            v_a = sb("v_a", [P, B, N_HEADS, HD + 1])
            v_b = sb("v_b", [P, B, 4, 4, HD + 1])
            qst = [sb(f"qst{i}", [P, NPAIR, UT], F16) for i in range(3)]
            qh, ql = sb("qh", [P, KC, UT], F16), sb("ql", [P, KC, UT], F16)
            stats, mv = sb("stats", [P, 2, 6]), sb("mv", [P, 2, 2])
            mv1, rstd1 = sb("mv1", [P, T, 2]), sb("rstd1", [P, T])
            var, rstd, newton = sb("var", [P, 2]), sb("rstd", [P, 2]), sb("newton", [P, 2])
            half_bits = sb("half_bits", [P, 2], I32)
            xn, xnT = sb("xn", [P, 2, D]), sb("xnT", [P, KC, UT])
            rowmax, negmax = sb("rowmax", [P, 2 * N_HEADS]), sb("negmax", [P, 2 * N_HEADS])
            negmaxT = sb("negmaxT", [2 * N_HEADS, P], F16)
            probs = sb("probs", [P, 3, 2, UT])
            recip = sb("recip", [P, 2, N_HEADS])
            attn, attnT = sb("attn", [P, 2, D]), sb("attnT", [P, 2, KC, P])
            xn2 = sb("xn2", [P, 2, D])
            xn2T = attnT
            es = outer

        with ExitStack() as es_route:
            outer, es = es, es_route
            before = sb("before", [P, P], F16)
            ones = sb("ones", [P, P], F16)
            iota_slot, iota_tile = sb("iota_slot", [P, P]), sb("iota_tile", [P, TAB])
            token_no, spare_row = sb("token_no", [P, TOP_K * T]), sb("spare_row", [P, 1])
            lower = sb("lower", [P, E, E])
            exp_z, sig = sb("exp_z", [P, T, E]), sb("sig", [P, T, E])
            ahead, tie = sb("ahead", [P, T, E, E]), sb("tie", [P, T, E, E])
            rank = sb("rank", [P, T * E])
            chosen = sb("chosen", [P, TOP_K, T * E])
            chosen16 = sb("chosen16", [P, T * E], F16)
            combine = sb("combine", [P, T, E])
            combineT = sb("combineT", [E, T, P])
            n_int, n_tiles, tile_end, tile_base, no_add = (sb("n_int", [P, E], I32), sb("n_tiles", [P, E]), sb("tile_end", [P, E]),
                                                            sb("tile_base", [P, E]), sb("no_add", [P, E]))
            slot_e = sb("slot_e", [P, T * E])
            picked = sb("picked", [P, TOP_K, T * E])
            slot, gate = sb("slot", [P, TOP_K * T]), sb("gate", [P, TOP_K * T])
            slot_i, tile_i, place_i = (sb(n, [P, TOP_K * T], I32) for n in ("slot_i", "tile_i", "place_i"))
            tile_f, place_f = sb("tile_f", [P, TOP_K * T]), sb("place_f", [P, TOP_K * T])
            at_place = sb("at_place", [P, TOP_K * T, P])
            tab_rhs = sb("tab_rhs", [P, TOP_K * T, 2, TAB])
            empty, token_m1 = sb("empty", [P, TAB]), sb("token_m1", [P, TAB])
            past = sb("past", [1, TAB, E])
            expert_f = sb("expert_f", [1, TAB])
            es = outer
        xg = [sb(f"xg{i}", [P, D]) for i in range(2)]
        gather_col = [sb(f"gather_col{i}", [P, 1], I32) for i in range(2)]
        scatter_col = [sb(f"scatter_col{i}", [P, 1], I32) for i in range(2)]
        xh, xl = ([sb(f"{n}{i}", [P, KC * P], F16) for i in range(2)] for n in ("xh", "xl"))
        h32 = [sb(f"h32_{i}", [P, FC * P]) for i in range(2)]
        hh, hl = ([sb(f"{n}{i}", [P, FC * P], F16) for i in range(2)] for n in ("hh", "hl"))
        y_sb = [sb(f"y_sb{i}", [P, D]) for i in range(2)]

        bank = [es.enter_context(nc.psum_tensor(f"bank{i}", [P, 512], F32)) for i in range(8)]
        XT_BANKS, Y_BANKS, H_BANKS = bank[4:6], bank[6:8], (bank[0:2], bank[2:4])
        INIT_BANKS = (bank[0], bank[1], bank[3], bank[6])
        S2_BANKS, PV_BANKS, A_BANK, Q_BANK, S1_BANKS = bank[0:2], bank[2:4], bank[4], bank[5], bank[6:8]

        x_loaded = [sem(f"x_loaded{u}") for u in range(U)]
        ctx_loaded, w_loaded, bias_loaded = sem("ctx_loaded"), sem("w_loaded"), sem("bias_loaded")
        zeroed, consts_made, select_made = sem("zeroed"), sem("consts_made"), sem("select_made")
        mask_row_made, tanh_made = sem("mask_row_made"), sem("tanh_made")
        setup_filled, setup_evac_act, setup_evac_dve = sem("setup_filled"), sem("setup_evac_act"), sem("setup_evac_dve")
        kv_filled, kv_made, kst_landed, kst_mid_landed, mask_made = sem("kv_filled"), sem("kv_made"), sem("kst_landed"), sem("kst_mid_landed"), sem("mask_made")
        v_made, ctx_late_made, kst_late_made = sem("v_made"), sem("ctx_late_made"), sem("kst_late_made")
        bo_gated = sem("bo_gated")
        dve_step = sem("dve_step")
        ln1_done, x_biased = sem("ln1_done"), sem("x_biased")
        a_filled, a_evac, q_filled, q_high, q_free = sem("a_filled"), sem("a_evac"), sem("q_filled"), sem("q_high"), sem("q_free")
        qst_landed = [sem(f"qst_landed{i}") for i in range(3)]
        max_landed = [sem(f"max_landed{i}") for i in range(3)]
        s1_filled, rowmax_done, negmax_done = sem("s1_filled"), sem("rowmax_done"), sem("negmax_done")
        s2_filled, exp_done, pv_done, attn_normed = sem("s2_filled"), sem("exp_done"), sem("pv_done"), sem("attn_normed")
        x2_done, ln2_done = sem("x2_done"), sem("ln2_done")
        xn2_stored = sem("xn2_stored")
        consts2_made = sem("consts2_made")
        w_staged, w_used, w_ready = [sem("w_staged0"), sem("w_staged1")], sem("w_used"), sem("w_ready")
        w_high = sem("w_high")
        exp_z_made, chosen_made, comb_made = sem("exp_z_made"), sem("chosen_made"), sem("comb_made")
        ranked, combT_filled, combT_made = sem("ranked"), sem("combT_filled"), sem("combT_made")
        at_place_made, tab_filled, tables_made = sem("at_place_made"), sem("tab_filled"), sem("tables_made")
        init_filled, init_added, init_stored = sem("init_filled"), sem("init_added"), sem("init_stored")
        cols_made, gather_issued, scatter_issued = sem("cols_made"), sem("gather_issued"), sem("scatter_issued")
        gathered = [sem("gathered0"), sem("gathered1")]
        xt_filled, xh_made, xl_made = sem("xt_filled"), sem("xh_made"), sem("xl_made")
        h_filled, gelu_done, hh_made, hl_made = sem("h_filled"), sem("gelu_done"), sem("hh_made"), sem("hl_made")
        y_filled, y_half_made, y_made, scattered = sem("y_filled"), sem("y_half_made"), sem("y_made"), sem("scattered")

        ITEMS = NPAIR + 2
        MAX_ITEMS = 3
        FRAMES = range(-2, U + 1)

        def live(u):
            return 0 <= u < U

        A_USES = [(k, u + d) for u in FRAMES for k, d in (("xT", 2), ("attnT", -1), ("maxT", 1), ("xn2T", -1)) if live(u + d)]
        Q_USES = [(k, u + d) for u in FRAMES for k, d in (("q", 2), ("wo", -1), ("logits", -1)) if live(u + d)]
        a_nth = {use: n + 1 for n, use in enumerate(A_USES)}
        q_nth = {use: n + 1 for n, use in enumerate(Q_USES)}
        QST_PER_USE, MAX_PER_USE = 12 * 16, 2 * 16
        KST_LANDED, KST_MID_LANDED = 16 * 8 * 2 * KC, 16 * 8 * KC

        def item_heads(i):
            return ("pair", i if i < 4 else i - 1) if i % 5 != 4 else ("late", i // 5)

        chunks = [(w1[e, k * P:(k + 1) * P, :], W1H, W1L, (e * KC + k) * F) for e in range(E) for k in range(KC)]
        chunks += [(w2[e, k * P:(k + 4) * P, :].rearrange("(c p) d -> p c d", p=P), W2[:, 0, :], W2[:, 1, :], (e * FC + k) * D)
                   for e in range(E) for k in range(0, FC, 4)]
        W_SLOTS = {u: tuple(range(2 * (u + 3), ITEMS)) if u < 0 else (1, 2, 3, 4, 6, 7) for u in FRAMES}
        w_steps = [(u, i) for u in FRAMES for i in W_SLOTS[u]]
        assert len(w_steps) >= 2 * len(chunks)
        first_chunk = {u + 2: w_steps.index((u, W_SLOTS[u][0])) // 2 for u in FRAMES if live(u + 2)}
        bias_at = {n: u for u, n in first_chunk.items()}

        def stack_keys(engine, grp, src, c, landed):
            for r in range(8):
                row = 32 * grp + 16 * (r % 2)
                engine.dma_start(kst[row:row + 16, :, 4 * c + r // 2, r % 2, 0:S],
                                 src[16 * r:16 * r + 16, c, :].rearrange("p (b s) -> p b s", b=B)).then_inc(landed, 16)

        block = es.enter_context(nc.Block())

        @block.sync
        def _(sp):
            sp.dma_start(ctx_a[:, :, :], ctx[:, 0:P, :].rearrange("b s d -> s b d")).then_inc(ctx_loaded, 16)
            sp.dma_start(ctx_b[:, :, :], ctx[:, P:S, :].rearrange("b s d -> s b d")).then_inc(ctx_loaded, 16)
            for u in range(2):
                sp.dma_start(X[:, 2 * u:2 * u + 2, :], x_t[:, 2 * u:2 * u + 2, :]).then_inc(x_loaded[u], 16)
            for n, w in enumerate((wq, wk, wv, wo)):
                sp.dma_start(W_nat[:, n, :, :], w.rearrange("(c p) d -> p c d", p=P)).then_inc(w_loaded, 16)
            for u in range(2, U):
                sp.dma_start(X[:, 2 * u:2 * u + 2, :], x_t[:, 2 * u:2 * u + 2, :]).then_inc(x_loaded[u], 16)
            sp.wait_ge(zeroed, 2)
            for c in range(KC):
                for grp, src in ((0, kh), (2, kl)):
                    sp.wait_ge(kv_made, 2 * c + grp // 2 + 1)
                    stack_keys(sp, grp, src, c, kst_landed)
            for u in FRAMES:
                if live(u + 2):
                    v = u + 2
                    if v >= 3:
                        sp.wait_ge(s2_filled, ITEMS * (v - 2))
                    sp.wait_ge(q_high, v + 1)
                    for grp in (0, 2):
                        for r in range(4):
                            sp.dma_start(qst[v % 3][32 * grp:32 * grp + 32, r:NPAIR:4, :],
                                         qh[32 * r:32 * r + 32, :, :]).then_inc(qst_landed[v % 3], 16)
                    sp.wait_ge(q_free, q_nth["q", v])
                    for r in range(4):
                        sp.dma_start(qst[v % 3][32:64, r:NPAIR:4, :],
                                     ql[32 * r:32 * r + 32, :, :]).then_inc(qst_landed[v % 3], 16)
                if live(u + 1):
                    v = u + 1
                    sp.wait_ge(a_evac, a_nth["maxT", v])
                    for j in range(2):
                        sp.dma_start(qst[v % 3][ROW_MAX:ROWS, :, j * P:(j + 1) * P],
                                     negmaxT[16 * j:16 * j + 16, :].unsqueeze(1).broadcast_to([16, NPAIR, P])
                                     ).then_inc(max_landed[v % 3], 16)
                if live(u - 1):
                    v = u - 1
                    sp.wait_ge(ln2_done, v + 1)
                    sp.dma_start(xn2_t[:, 2 * v:2 * v + 2, :], xn2[:, :, :]).then_inc(xn2_stored, 16)
            for q in range(4):
                sp.wait_ge(init_added, 2 * q + 2)
                sp.dma_start(out_t[:, 4 * q:4 * q + 4, :], X[:, 4 * q:4 * q + 4, :]).then_inc(init_stored, 16)
            sp.dma_start(out[N:N + P, :], X[:, 0, :]).then_inc(init_stored, 16)
            sp.wait_ge(init_stored, 16 * 5)

        @block.gpsimd
        def _(pool):
            nc.gpsimd.memset(kst[:, 0, :, :, :], 0.0).then_inc(zeroed, 1)
            nc.gpsimd.memset(kst[:, 1, :, :, :], 0.0).then_inc(zeroed, 1)
            nc.gpsimd.memset(ident[:, :], 0.0).then_inc(zeroed, 1)
            nc.gpsimd.memset(pad_mask[:, :], 1.0).then_inc(zeroed, 1)
            pool.wait_ge(zeroed, 4)
            nc.gpsimd.affine_select(out=ident[:, :], in_=ident[:, :], compare_op=ALU.not_equal, fill=1.0, base=0,
                                    pattern=[[-1, P]], channel_multiplier=1).then_inc(consts_made, 1)
            for j in range(4):
                pool.wait_ge(consts_made, j + 1)
                part = pad_mask[32 * j:32 * j + 32, :]
                nc.gpsimd.affine_select(out=part, in_=part, compare_op=ALU.is_ge, fill=0.0, base=S2 - 1,
                                        pattern=[[0, 1]], channel_multiplier=-1).then_inc(consts_made, 1)
            pool.wait_ge(consts_made, 5)
            for b in range(B):
                if b:
                    pool.wait_ge(select_made, b)
                sel = kst[ROW_ONE:ROW_ONE + 32, b, :, :, 0:S].rearrange("p n a s -> p (n a) s")
                nc.gpsimd.affine_select(out=sel, in_=sel, compare_op=ALU.not_equal, fill=1.0, base=-1,
                                        pattern=[[-1, N_HEADS], [0, S]], channel_multiplier=1).then_inc(select_made, 1)
            def load(n):
                src = chunks[n][0]
                dst = W_stage[n % 2][:, :]
                if len(src.shape) == 3:
                    dst = dst.rearrange("p (c d) -> p c d", c=4)
                pool.dma_start(dst, src).then_inc(w_staged[n % 2], 16)

            load(0)
            load(1)
            for c in range(KC):
                pool.wait_ge(kv_made, 2 * c + 1)
                stack_keys(pool, 1, kh, c, kst_mid_landed)
            pool.wait_ge(bo_gated, 1)
            for n, (_, high, low, at) in enumerate(chunks):
                stage = W_stage[n % 2]
                if n in bias_at:
                    u = bias_at[n]
                    pool.wait_ge(ln1_done, u + 1)
                    nc.gpsimd.tensor_tensor(X[:, 2 * u:2 * u + 2, :], X[:, 2 * u:2 * u + 2, :],
                                            bias_o[:, :].unsqueeze(1).broadcast_to([P, 2, D]), ALU.add).then_inc(x_biased, 1)
                pool.wait_ge(w_high, n + 1)
                if n == E * KC:
                    pool.wait_ge(kst_late_made, 1)
                nc.gpsimd.tensor_tensor(low[:, at:at + W_CHUNK], stage[:, :], high[:, at:at + W_CHUNK], ALU.subtract).then_inc(w_ready, 1)
                if n + 2 < len(chunks):
                    pool.wait_ge(w_ready, n + 1)
                    load(n + 2)

            pool.wait_ge(q_free, len(Q_USES))
            pool.wait_ge(xn2_stored, 16 * U)
            nc.gpsimd.memset(ones[:, :], 1.0).then_inc(consts2_made, 1)
            nc.gpsimd.memset(before[:, :], 1.0).then_inc(consts2_made, 1)
            nc.gpsimd.memset(lower[:, :, :], 1.0).then_inc(consts2_made, 1)
            pool.wait_ge(consts2_made, 3)
            nc.gpsimd.affine_select(out=before[:, :], in_=before[:, :], compare_op=ALU.is_gt, fill=0.0, base=0,
                                    pattern=[[1, P]], channel_multiplier=-1).then_inc(consts2_made, 1)
            nc.gpsimd.affine_select(out=lower[:, :, :], in_=lower[:, :, :], compare_op=ALU.is_gt, fill=0.0, base=0,
                                    pattern=[[1, E], [-1, E]], channel_multiplier=0).then_inc(consts2_made, 1)
            exact = dict(allow_small_or_imprecise_dtypes=True)
            nc.gpsimd.iota(iota_slot[:, :], pattern=[[1, P]], base=0, channel_multiplier=0, **exact).then_inc(consts2_made, 1)
            nc.gpsimd.iota(iota_tile[:, :], pattern=[[1, TAB]], base=0, channel_multiplier=0, **exact).then_inc(consts2_made, 1)
            nc.gpsimd.iota(token_no[:, :], pattern=[[0, TOP_K], [P, T]], base=1, channel_multiplier=1, **exact).then_inc(consts2_made, 1)
            nc.gpsimd.iota(spare_row[:, :], pattern=[[0, 1]], base=N + 1, channel_multiplier=1, **exact).then_inc(consts2_made, 1)

            def gather(t, par):
                pool.wait_ge(cols_made, t + 1)
                pool.sem_inc(gather_issued, 1)
                nc.gpsimd.indirect_dma_start(out=xg[par][:, :], out_offset=None, in_=xn2_dram,
                                             in_offset=bass.IndirectOffsetOnAxis(ap=gather_col[par][:, 0:1], axis=0)
                                             ).then_inc(gathered[par], 16)

            def scatter(t, par, first=False):
                pool.wait_ge(y_made, t + 1)
                if not first:
                    pool.wait_ge(scattered, 16 * t)
                pool.sem_inc(scatter_issued, 1)
                nc.gpsimd.indirect_dma_start(out=out, out_offset=bass.IndirectOffsetOnAxis(ap=scatter_col[par][:, 0:1], axis=0),
                                             in_=y_sb[par][:, :], in_offset=None, compute_op=ALU.add).then_inc(scattered, 16)

            gather(0, 0)
            gather(1, 1)
            for t in range(2, 5):
                pool.wait_ge(xt_filled, t - 1)
                gather(t, t % 2)
            pool.wait_ge(init_stored, 16 * 5)

            def two_tiles(t, first=False):
                for d in range(2):
                    pool.wait_ge(xt_filled, t + (d + 3))
                    gather(t + (d + 4), 1 - d)
                    scatter(t + (d - 1), d, first=first and d == 0)

            two_tiles(1, first=True)
            with pool.Fori(0, LOOP) as pair:
                two_tiles(pair * 2 + 3)
            for t in range(NT - 3, NT):
                scatter(t, t % 2)
            pool.wait_ge(scattered, 16 * NT)
            for par in range(2):
                pool.wait_ge(gathered[par], 16 * ((TAB + 1 - par) // 2))

        BIAS_DMAS = 10

        @block.scalar
        def _(act):
            with nc.allow_non_contiguous_dma(reason="bias columns"):
                act.dma_start(bias_q[:, :], bq.rearrange("(c p) -> p c", p=P)).then_inc(bias_loaded, 16)
                act.dma_start(bias_k[:, :], bk.rearrange("(c p) -> p c", p=P)).then_inc(bias_loaded, 16)
            act.dma_start(bias_v[:, :], bv.partition_broadcast(P)).then_inc(bias_loaded, 16)
            act.dma_start(bias_o[:, :], bo.partition_broadcast(P)).then_inc(bias_loaded, 16)
            act.dma_start(gates[:, 0:1], g_xattn.partition_broadcast(P)).then_inc(bias_loaded, 16)
            act.dma_start(gates[:, 1:2], g_ffn.partition_broadcast(P)).then_inc(bias_loaded, 16)
            act.dma_start(mask_u8[:, :], mask.rearrange("b s -> (b s)").partition_broadcast(P)).then_inc(bias_loaded, 16)
            act.dma_start(wg_sb[:, :, :], wg.rearrange("(c p) e -> p c e", p=P)).then_inc(bias_loaded, 16)
            act.dma_start(b2_sb[:, :], b2).then_inc(bias_loaded, 16)
            act.dma_start(b1_nat[:, :], b1.rearrange("e (m p) -> (e m) p", p=P)).then_inc(bias_loaded, 16)
            act.wait_ge(bias_loaded, 16 * BIAS_DMAS)
            nc.scalar.activation(tanh_g[:, :], gates[:, :], ACT.Tanh).then_inc(tanh_made, 1)
            for n in (0, 2, 4, 6):
                act.wait_ge(setup_filled, n + 1)
                if n == 0:
                    ins = nc.scalar.activation(ctxT[:, :, 0, 0:S], bank[0][:, 0:KC * SP].rearrange("p (c s) -> p c s", c=KC)[:, :, 0:S], ACT.Copy)
                elif n == 6:
                    ins = nc.scalar.activation(b1T[:, :], bank[6][:, 0:E * FC], ACT.Copy)
                else:
                    ins = nc.scalar.activation({2: WT_kv[:, 0, :, :], 4: WT_qo[:, 0, :, :]}[n].rearrange("p c d -> p (c d)"), bank[n][:, :], ACT.Copy)
                ins.then_inc(setup_evac_act, 1)
            act.wait_ge(select_made, 2)
            act.wait_ge(mask_made, 1)
            for b in range(B):
                nc.scalar.activation(kst[ROW_ONE:ROW_ONE + 1, b, :, :, 0:S].rearrange("p n a s -> p (n a) s"),
                                     mask_f[ROW_ONE:ROW_ONE + 1, b * S:(b + 1) * S].unsqueeze(1).broadcast_to([1, N_HEADS, S]),
                                     ACT.Copy, scale=-MASK_ADDEND, bias=MASK_ADDEND).then_inc(mask_row_made, 1)

            def weights_high(n, part):
                _, high, _, at = chunks[n]
                stage = W_stage[n % 2]
                if part == 0:
                    act.wait_ge(w_staged[n % 2], 16 * (n // 2 + 1))
                    nc.scalar.activation(high[:, at:at + W_CHUNK], stage[:, :], ACT.Copy, scale=W_SCALE)
                else:
                    nc.scalar.activation(stage[:, :], stage[:, :], ACT.Copy, scale=W_SCALE).then_inc(w_high, 1)

            for u in FRAMES:
                for i in range(ITEMS):
                    if live(u):
                        g = ITEMS * u + i
                        act.wait_ge(s2_filled, g + 1)
                        if g >= 3:
                            act.wait_ge(pv_done, g - 2)
                        nc.scalar.activation(probs[:, g % 3, :, :].rearrange("p a t -> p (a t)"), S2_BANKS[g % 2][:, :],
                                             ACT.Exp, scale=SCORE_SCALE).then_inc(exp_done, 1)
                    if i == 0 and live(u + 2):
                        v = u + 2
                        act.wait_ge(a_filled, a_nth["xT", v])
                        if v >= 1:
                            act.wait_ge(q_filled, q_nth["q", v - 1])
                        nc.scalar.activation(xnT[:, :, :].rearrange("p c t -> p (c t)"), A_BANK[:, :], ACT.Copy).then_inc(a_evac, 1)
                    if i == 2 and live(u - 1):
                        v = u - 1
                        act.wait_ge(a_filled, a_nth["attnT", v])
                        if v >= 1:
                            act.wait_ge(q_filled, q_nth["wo", v - 1])
                        nc.scalar.activation(attnT[:, :, :, :].rearrange("p j c t -> p (j c t)"), A_BANK[:, :], ACT.Copy).then_inc(a_evac, 1)
                    if i == 1 and live(u + 2):
                        v = u + 2
                        act.wait_ge(q_filled, q_nth["q", v])
                        if v >= 1:
                            act.wait_ge(qst_landed[(v - 1) % 3], QST_PER_USE * ((v - 1) // 3 + 1))
                        for c in range(KC):
                            ins = nc.scalar.activation(qh[:, c, :], Q_BANK[:, c * UT:(c + 1) * UT], ACT.Identity, bias=bias_q[:, c:c + 1])
                        ins.then_inc(q_high, 1)
                    if i == 6 and live(u + 1):
                        v = u + 1
                        act.wait_ge(a_filled, a_nth["maxT", v])
                        if v >= 1:
                            act.wait_ge(max_landed[(v - 1) % 3], MAX_PER_USE * ((v - 1) // 3 + 1))
                        nc.scalar.activation(negmaxT[:, :], A_BANK[0:2 * N_HEADS, 0:P], ACT.Copy).then_inc(a_evac, 1)
                    if i in W_SLOTS[u]:
                        n, part = divmod(w_steps.index((u, i)), 2)
                        if n < len(chunks):
                            weights_high(n, part)
                    if i == 8 and live(u - 1):
                        v = u - 1
                        act.wait_ge(a_filled, a_nth["xn2T", v])
                        if v >= 1:
                            act.wait_ge(q_filled, q_nth["logits", v - 1])
                        nc.scalar.activation(xn2T[:, :, :, :].rearrange("p j c t -> p (j c t)"), A_BANK[:, :], ACT.Copy).then_inc(a_evac, 1)

            act.wait_ge(q_free, len(Q_USES))
            act.wait_ge(xn2_stored, 16 * U)
            nc.scalar.activation(exp_z[:, :, :], Z[:, :, :], ACT.Exp, scale=-1.0).then_inc(exp_z_made, 1)
            for q in range(4):
                act.wait_ge(combT_filled, q + 1)
                nc.scalar.activation(combineT[:, 4 * q:4 * q + 4, :].rearrange("e t p -> e (t p)"), bank[3 + q][0:E, :], ACT.Copy).then_inc(combT_made, 1)

            def to_high(t, par):
                act.wait_ge(xt_filled, t + 1)
                nc.scalar.activation(xh[par][:, :], XT_BANKS[par][:, 0:KC * P], ACT.Copy).then_inc(xh_made, 1)

            def gelu(t, par, warm=True):
                column = act.value_load(bias_col[0:1, bass.ds(t, 1)], min_val=0, max_val=(E - 1) * FC)
                if warm:
                    act.wait_ge(hl_made, 2 * t - 2)
                for half in range(2):
                    act.wait_ge(h_filled, 2 * t + half + 1)
                    for m in range(FC // 2 * half, FC // 2 * (half + 1)):
                        ins = nc.scalar.activation(h32[par][:, m * P:(m + 1) * P], H_BANKS[par][half][:, m % 4 * P:(m % 4 + 1) * P],
                                                   ACT.Gelu_apprx_tanh, scale=1.0 / W_SCALE, bias=b1T[:, bass.ds(column + m, 1)])
                    ins.then_inc(gelu_done, 1)

            act.wait_ge(tables_made, 1)
            to_high(0, 0)
            to_high(1, 1)
            gelu(0, 0, warm=False)
            to_high(2, 0)
            gelu(1, 1, warm=False)

            def two_tiles(t):
                to_high(t + 2, 1)
                gelu(t + 1, 0)
                to_high(t + 3, 0)
                gelu(t + 2, 1)

            two_tiles(1)
            with act.Fori(0, LOOP) as pair:
                two_tiles(pair * 2 + 3)
            gelu(NT - 1, 0)

        @block.vector
        def _(dve):
            steps = [0]

            def step(ins):
                steps[0] += 1
                ins.then_inc(dve_step, 1)
                dve.wait_ge(dve_step, steps[0])

            for i in range(3):
                nc.vector.memset(qst[i][ROW_ONE:ROW_ONE + 1, :, :], 1.0)
            nc.vector.memset(ctxT[:, :, :, S:SP], 0.0)
            nc.vector.memset(v_a[:, :, :, :], 1.0)
            step(nc.vector.memset(v_b[:, :, :, :, :], 0.0))
            dve.wait_ge(consts_made, 5)
            for j in range(4):
                nc.vector.tensor_copy(v_b[32 * j:32 * j + 32, :, :, j, HD:HD + 1].rearrange("p b q d -> p (b q) d"),
                                      pad_mask[32 * j:32 * j + 32, :].unsqueeze(1).broadcast_to([32, 4 * B, 1]))
            dve.wait_ge(bias_loaded, 16 * BIAS_DMAS)
            nc.vector.tensor_copy(mask_f[:, :], mask_u8[:, :]).then_inc(mask_made, 1)
            nc.vector.tensor_scalar(bias_v_pad[:, :], bias_v[:, :], pad_mask[:, 0:1], None, ALU.mult)
            dve.wait_ge(tanh_made, 1)
            nc.vector.tensor_scalar(bias_o[:, :], bias_o[:, :], tanh_g[:, 0:1], None, ALU.mult).then_inc(bo_gated, 1)
            for n in (1, 3, 5):
                dve.wait_ge(setup_filled, n + 1)
                if n == 1:
                    ins = nc.vector.tensor_copy(ctxT[:, :, 1, 0:S], bank[1][:, 0:KC * SP].rearrange("p (c s) -> p c s", c=KC)[:, :, 0:S])
                else:
                    ins = nc.vector.tensor_copy({3: WT_kv[:, 1, :, :], 5: WT_qo[:, 1, :, :]}[n].rearrange("p c d -> p (c d)"), bank[n][:, :])
                ins.then_inc(setup_evac_dve, 1)
            dve.wait_ge(setup_evac_act, 1)
            dve.wait_ge(setup_evac_dve, 1)
            nc.vector.tensor_copy(ctxT_late[:, :, :, :, :].rearrange("p k b j s -> p (k b) j s"),
                                  ctxT[:, :, :, P:SP].rearrange("p k b s -> p (k b) s").unsqueeze(2).broadcast_to([P, KC * B, 4, SP - P])
                                  ).then_inc(ctx_late_made, 1)
            dve.wait_ge(mask_made, 1)
            for c in range(KC):
                dve.wait_ge(kv_filled, c + 1)
                step(nc.vector.scalar_tensor_tensor(out=kf[:, c, :], in0=bank[c][:, 0:B * S], scalar=bias_k[:, c:c + 1],
                                                    in1=mask_f[:, :], op0=ALU.add, op1=ALU.mult))
                nc.vector.tensor_copy(kh[:, c, :], kf[:, c, :]).then_inc(kv_made, 1)
                dve.wait_ge(kv_made, 2 * c + 1)
                nc.vector.tensor_tensor(kl[:, c, :], kf[:, c, :], kh[:, c, :], ALU.subtract).then_inc(kv_made, 1)
            dve.wait_ge(kv_filled, 3)
            nc.vector.tensor_tensor(v_a[:, :, :, 0:HD], bank[2][:, :].rearrange("p (b h d) -> p b h d", b=B, h=N_HEADS),
                                    bias_v[:, :].rearrange("p (h d) -> p h d", h=N_HEADS).unsqueeze(1).broadcast_to([P, B, N_HEADS, HD]),
                                    ALU.add).then_inc(v_made, 1)
            dve.wait_ge(kv_filled, 4)
            for b in range(B):
                for j in range(4):
                    rows = slice(32 * j, 32 * j + 32)
                    ins = nc.vector.scalar_tensor_tensor(
                        out=v_b[rows, b, :, j, 0:HD],
                        in0=bank[3][rows, b * D:(b + 1) * D].rearrange("p (q j d) -> p q j d", q=4, j=4)[:, :, j, :],
                        scalar=pad_mask[rows, 0:1],
                        in1=bias_v_pad[rows, :].rearrange("p (q j d) -> p q j d", q=4, j=4)[:, :, j, :],
                        op0=ALU.mult, op1=ALU.add)
            ins.then_inc(v_made, 1)

            dve.wait_ge(kst_landed, KST_LANDED)
            dve.wait_ge(kst_mid_landed, KST_MID_LANDED)
            dve.wait_ge(mask_row_made, B)
            nc.vector.tensor_copy(kst_late[:, :, :, :].rearrange("p b n (a s) -> p (b n a) s", a=2),
                                  kst[:, :, :, :, P:SP].rearrange("p b n a s -> p (b n a) s")).then_inc(kst_late_made, 1)

            def row_stats(src, n, stats, mv, var, rstd, newton, half_bits):
                for j in range(n):
                    ins = nc.vector.bn_stats(stats[:, j, :], src[:, j, :])
                step(ins)
                for j in range(n):
                    ins = nc.vector.bn_aggr(mv[:, j, :], stats[:, j, :])
                step(ins)
                step(nc.vector.tensor_scalar(var[:, :], mv[:, :, 1], EPS, None, ALU.add))
                step(nc.vector.tensor_scalar(half_bits[:, :], var[:, :].bitcast(I32), 1, None, ALU.logical_shift_right))
                nc.vector.tensor_scalar(var[:, :], var[:, :], -0.5, None, ALU.mult)
                step(nc.vector.tensor_scalar(rstd[:, :].bitcast(I32), half_bits[:, :], -1, RSQRT_MAGIC, ALU.mult, ALU.add))
                for _ in range(3):
                    step(nc.vector.tensor_tensor(newton[:, :], rstd[:, :], rstd[:, :], ALU.mult))
                    step(nc.vector.tensor_tensor(newton[:, :], newton[:, :], var[:, :], ALU.mult))
                    step(nc.vector.scalar_tensor_tensor(out=rstd[:, :], in0=newton[:, :], scalar=1.5, in1=rstd[:, :], op0=ALU.add, op1=ALU.mult))

            def normalise(dst, src, mv, rstd):
                for j in range(2):
                    ins = nc.vector.tensor_scalar(dst[:, j, :], src[:, j, :], mv[:, j, 0:1], rstd[:, j:j + 1], ALU.subtract, ALU.mult)
                return ins

            def layernorm1(v):
                if v >= 1:
                    dve.wait_ge(a_filled, a_nth["xT", v - 1])
                normalise(xn, X[:, 2 * v:2 * v + 2, :], mv1[:, 2 * v:2 * v + 2, :], rstd1[:, 2 * v:2 * v + 2]).then_inc(ln1_done, 1)

            for u in range(U):
                dve.wait_ge(x_loaded[u], 16)
            row_stats(X, T, stats1, mv1, var1, rstd1, newton1, half_bits1)
            layernorm1(0)

            for u in FRAMES:
                for i in range(ITEMS):
                    if i == 0 and live(u - 1):
                        v = u - 1
                        dve.wait_ge(pv_done, ITEMS * (v + 1))
                        if v >= 1:
                            dve.wait_ge(a_filled, a_nth["attnT", v - 1])
                        pv = [PV_BANKS[j][:, 0:N_HEADS * (HD + 1)].rearrange("p (h d) -> p h d", h=N_HEADS) for j in range(2)]
                        for j in range(2):
                            ins = nc.vector.reciprocal(recip[:, j, :].unsqueeze(2), pv[j][:, :, HD:HD + 1])
                        step(ins)
                        for j in range(2):
                            nc.vector.tensor_tensor(attn[:, j, :].rearrange("p (h d) -> p h d", h=N_HEADS), pv[j][:, :, 0:HD],
                                                    recip[:, j, :].unsqueeze(2).broadcast_to([P, N_HEADS, HD]),
                                                    ALU.mult).then_inc(attn_normed, 1)
                    if live(u + 1):
                        for n in range(MAX_ITEMS * i, min(MAX_ITEMS * (i + 1), 2 * NPAIR)):
                            g = 2 * NPAIR * (u + 1) + n
                            dve.wait_ge(s1_filled, g + 1)
                            nc.vector.reduce_max(rowmax[:, 2 * n:2 * n + 2],
                                                 S1_BANKS[g % 2][:, 0:2 * S].rearrange("p (a s) -> p a s", a=2),
                                                 AX_X).then_inc(rowmax_done, 1)
                    if i == 2 and live(u + 2):
                        v = u + 2
                        dve.wait_ge(q_high, v + 1)
                        if v >= 1:
                            dve.wait_ge(qst_landed[(v - 1) % 3], QST_PER_USE * ((v - 1) // 3 + 1))
                        for c in range(KC):
                            ins = nc.vector.scalar_tensor_tensor(out=ql[:, c, :], in0=Q_BANK[:, c * UT:(c + 1) * UT], scalar=bias_q[:, c:c + 1],
                                                                 in1=qh[:, c, :], op0=ALU.add, op1=ALU.subtract)
                        ins.then_inc(q_free, 1)
                    if i == 4 and live(u - 1):
                        v = u - 1
                        dve.wait_ge(q_filled, q_nth["wo", v])
                        dve.wait_ge(x_biased, v + 1)
                        unit = X[:, 2 * v:2 * v + 2, :].rearrange("p j d -> p (j d)")
                        nc.vector.scalar_tensor_tensor(out=unit, in0=Q_BANK[:, :], scalar=tanh_g[:, 0:1], in1=unit,
                                                       op0=ALU.mult, op1=ALU.add).then_inc(q_free, 1)
                    if i == 5 and live(u + 1):
                        v = u + 1
                        dve.wait_ge(rowmax_done, 2 * NPAIR * (v + 1))
                        if v >= 1:
                            dve.wait_ge(a_filled, a_nth["maxT", v - 1])
                        nc.vector.tensor_scalar(negmax[:, :], rowmax[:, :], -1.0, None, ALU.mult).then_inc(negmax_done, 1)
                    if i == 5 and live(u - 1):
                        v = u - 1
                        dve.wait_ge(q_free, q_nth["wo", v])
                        if v >= 1:
                            dve.wait_ge(xn2_stored, 16 * v)
                            dve.wait_ge(a_filled, a_nth["xn2T", v - 1])
                        unit = X[:, 2 * v:2 * v + 2, :]
                        row_stats(unit, 2, stats, mv, var, rstd, newton, half_bits)
                        normalise(xn2, unit, mv, rstd).then_inc(ln2_done, 1)
                    if i == 7 and live(u + 3):
                        layernorm1(u + 3)
                    if i == 9 and live(u - 1):
                        v = u - 1
                        dve.wait_ge(q_filled, q_nth["logits", v])
                        nc.vector.tensor_copy(Z[:, 2 * v:2 * v + 2, :].rearrange("p j e -> p (j e)"), Q_BANK[:, 0:2 * E]).then_inc(q_free, 1)
            dve.wait_ge(exp_z_made, 1)
            step(nc.vector.tensor_scalar(exp_z[:, :, :], exp_z[:, :, :], 1.0, None, ALU.add))
            step(nc.vector.reciprocal(sig[:, :, :], exp_z[:, :, :]))
            mine = sig[:, :, :].unsqueeze(3).broadcast_to([P, T, E, E])
            other = sig[:, :, :].unsqueeze(2).broadcast_to([P, T, E, E])
            nc.vector.tensor_tensor(ahead[:, :, :, :], other, mine, ALU.is_gt)
            step(nc.vector.tensor_tensor(tie[:, :, :, :], other, mine, ALU.is_equal))
            dve.wait_ge(consts2_made, 9)
            flat = "p t a b -> p t (a b)"
            step(nc.vector.tensor_tensor(tie[:, :, :, :].rearrange(flat), tie[:, :, :, :].rearrange(flat),
                                         lower[:, :, :].rearrange("p a b -> p (a b)").unsqueeze(1).broadcast_to([P, T, E * E]), ALU.mult))
            step(nc.vector.tensor_tensor(ahead[:, :, :, :].rearrange(flat), ahead[:, :, :, :].rearrange(flat), tie[:, :, :, :].rearrange(flat), ALU.add))
            step(nc.vector.reduce_sum(rank[:, :], ahead[:, :, :, :].rearrange("p t a b -> p (t a) b"), AX_X))
            nc.vector.tensor_scalar(chosen16[:, :], rank[:, :], float(TOP_K), None, ALU.is_lt).then_inc(chosen_made, 1)
            for k in range(TOP_K):
                nc.vector.tensor_scalar(chosen[:, k, :], rank[:, :], float(k), None, ALU.is_equal)
            dve.wait_ge(chosen_made, 1)
            nc.vector.tensor_tensor(combine[:, :, :].rearrange("p t e -> p (t e)"), sig[:, :, :].rearrange("p t e -> p (t e)"),
                                    chosen16[:, :], ALU.mult).then_inc(comb_made, 1)
            dve.wait_ge(ranked, 2)
            nc.vector.memset(no_add[:, :], 0.0)
            step(nc.vector.tensor_scalar(n_int[:, :], bank[1][:, 0:E], float(P - 1), None, ALU.add))
            step(nc.vector.tensor_scalar(n_int[:, :], n_int[:, :], 7, None, ALU.logical_shift_right))
            step(nc.vector.tensor_copy(n_tiles[:, :], n_int[:, :]))
            step(nc.vector.tensor_tensor_scan(out=tile_end[:, :], data0=n_tiles[:, :], data1=no_add[:, :], initial=0.0, op0=ALU.add, op1=ALU.add))
            step(nc.vector.tensor_tensor(tile_base[:, :], tile_end[:, :], n_tiles[:, :], ALU.subtract))
            step(nc.vector.tensor_scalar(tile_base[:, :], tile_base[:, :], float(P), None, ALU.mult))
            step(nc.vector.tensor_tensor(slot_e[:, :].rearrange("p (t e) -> p t e", e=E), bank[0][:, 0:T * E].rearrange("p (t e) -> p t e", e=E),
                                         tile_base[:, :].unsqueeze(1).broadcast_to([P, T, E]), ALU.add))
            for src, dst in ((slot_e[:, :], slot), (sig[:, :, :].rearrange("p t e -> p (t e)"), gate)):
                step(nc.vector.tensor_tensor(picked[:, :, :], chosen[:, :, :], src.unsqueeze(1).broadcast_to([P, TOP_K, T * E]), ALU.mult))
                step(nc.vector.reduce_sum(dst[:, :], picked[:, :, :].rearrange("p k (t e) -> p (k t) e", e=E), AX_X))
            step(nc.vector.tensor_copy(slot_i[:, :], slot[:, :]))
            nc.vector.tensor_scalar(tile_i[:, :], slot_i[:, :], 7, None, ALU.logical_shift_right)
            step(nc.vector.tensor_scalar(place_i[:, :], slot_i[:, :], P - 1, None, ALU.bitwise_and))
            nc.vector.tensor_copy(tile_f[:, :], tile_i[:, :])
            step(nc.vector.tensor_copy(place_f[:, :], place_i[:, :]))
            M = TOP_K * T
            step(nc.vector.tensor_tensor(tab_rhs[:, :, 0, :], tile_f[:, :].unsqueeze(2).broadcast_to([P, M, TAB]),
                                         iota_tile[:, :].unsqueeze(1).broadcast_to([P, M, TAB]), ALU.is_equal))
            for n, val in ((1, gate), (0, token_no)):
                nc.vector.tensor_tensor(tab_rhs[:, :, n, :], tab_rhs[:, :, 0, :], val[:, :].unsqueeze(2).broadcast_to([P, M, TAB]), ALU.mult)
            for n in range(0, M, PLACES):
                nc.vector.tensor_tensor(at_place[:, n:n + PLACES, :], place_f[:, n:n + PLACES].unsqueeze(2).broadcast_to([P, PLACES, P]),
                                        iota_slot[:, :].unsqueeze(1).broadcast_to([P, PLACES, P]), ALU.is_equal).then_inc(at_place_made, 1)
            step(nc.vector.tensor_tensor(past[:, :, :], iota_tile[0:1, :].unsqueeze(2).broadcast_to([1, TAB, E]),
                                    tile_end[0:1, :].unsqueeze(1).broadcast_to([1, TAB, E]), ALU.is_ge))
            step(nc.vector.reduce_sum(expert_f[:, :], past[:, :, :], AX_X))
            nc.vector.tensor_scalar(weight_col[:, :], expert_f[:, :], float(E - 1), float(KC * F), ALU.min, ALU.mult)
            nc.vector.tensor_scalar(bias_col[:, :], expert_f[:, :], float(E - 1), float(FC), ALU.min, ALU.mult)
            dve.wait_ge(tab_filled, 1)
            nc.vector.tensor_scalar(empty[:, :], bank[2][:, 0:TAB], 0.0, None, ALU.is_equal)
            nc.vector.tensor_scalar(token_m1[:, :], bank[2][:, 0:TAB], -1.0, None, ALU.add)
            nc.vector.tensor_scalar(gather_tab[:, :], bank[2][:, 0:TAB], -1.0, 0.0, ALU.add, ALU.max)
            step(nc.vector.tensor_scalar(gate_tab[:, :], bank[2][:, TAB:2 * TAB], tanh_g[:, 1:2], 1.0 / W_SCALE, ALU.mult, ALU.mult))
            nc.vector.scalar_tensor_tensor(out=scatter_tab[:, :], in0=empty[:, :], scalar=spare_row[:, 0:1], in1=token_m1[:, :],
                                           op0=ALU.mult, op1=ALU.add).then_inc(tables_made, 1)
            def cols(t, par, warm=True):
                if warm:
                    dve.wait_ge(scattered, 16 * (t - 1))
                nc.vector.tensor_copy(scatter_col[par][:, :], scatter_tab[:, bass.ds(t, 1)])

            def gather_cols(t, par, wait):
                if wait is not None:
                    dve.wait_ge(gathered[par], wait)
                nc.vector.tensor_copy(gather_col[par][:, :], gather_tab[:, bass.ds(t, 1)]).then_inc(cols_made, 1)

            def to_low(t, par):
                dve.wait_ge(xh_made, t + 1)
                nc.vector.tensor_tensor(xl[par][:, :], XT_BANKS[par][:, 0:KC * P], xh[par][:, :], ALU.subtract).then_inc(xl_made, 1)

            def split_h(t, par, half, warm=True):
                cut = slice(FC // 2 * P * half, FC // 2 * P * (half + 1))
                dve.wait_ge(gelu_done, 2 * t + half + 1)
                if warm and half == 0:
                    dve.wait_ge(y_filled, t - 1)
                nc.vector.tensor_copy(hh[par][:, cut], h32[par][:, cut]).then_inc(hh_made, 1)
                dve.wait_ge(hh_made, 2 * t + half + 1)
                nc.vector.tensor_tensor(hl[par][:, cut], h32[par][:, cut], hh[par][:, cut], ALU.subtract).then_inc(hl_made, 1)

            def weigh_y(t, par, warm=True):
                dve.wait_ge(y_filled, t + 1)
                cols(t, par, warm)
                gate = gate_tab[:, bass.ds(t, 1)]
                nc.vector.tensor_scalar(y_sb[par][:, :], Y_BANKS[par][:, 0:D], gate, None, ALU.mult).then_inc(y_half_made, 1)
                dve.wait_ge(y_half_made, t + 1)
                nc.vector.scalar_tensor_tensor(out=y_sb[par][:, :], in0=Y_BANKS[par][:, D:2 * D], scalar=gate, in1=y_sb[par][:, :],
                                               op0=ALU.mult, op1=ALU.add).then_inc(y_made, 1)

            dve.wait_ge(tables_made, 1)
            gather_cols(0, 0, None)
            gather_cols(1, 1, None)
            for u in range(U):
                dve.wait_ge(init_filled, u + 1)
                unit = X[:, 2 * u:2 * u + 2, :].rearrange("p j d -> p (j d)")
                nc.vector.scalar_tensor_tensor(out=unit, in0=INIT_BANKS[u % 4][:, :], scalar=tanh_g[:, 1:2], in1=unit,
                                               op0=ALU.mult, op1=ALU.add).then_inc(init_added, 1)
            gather_cols(2, 0, 16)
            to_low(0, 0)
            to_low(1, 1)
            gather_cols(3, 1, 16)
            split_h(0, 0, 0, warm=False)
            gather_cols(4, 0, 32)
            split_h(0, 0, 1, warm=False)
            to_low(2, 0)
            split_h(1, 1, 0, warm=False)

            def iteration(t, par, wait, warm=True):
                weigh_y(t - 1, 1 - par, warm=warm)
                gather_cols(t + 4, par, wait)
                split_h(t, par, 1)
                to_low(t + 2, par)
                split_h(t + 1, 1 - par, 0)

            def two_tiles(t, first=False):
                iteration(t, 1, 8 * (t + 1) + 16, warm=not first)
                iteration(t + 1, 0, 8 * (t + 1) + 32, warm=not first)

            two_tiles(1, first=True)
            with dve.Fori(0, LOOP) as pair:
                two_tiles(pair * 2 + 3)
            weigh_y(NT - 3, 0)
            split_h(NT - 2, 1, 1)
            split_h(NT - 1, 0, 0)
            weigh_y(NT - 2, 1)
            split_h(NT - 1, 0, 1)
            weigh_y(NT - 1, 0)

        @block.tensor
        def _(pe):
            pe.wait_ge(consts_made, 1)
            pe.wait_ge(ctx_loaded, 32)
            for b in range(B):
                for c in range(KC):
                    nc.tensor.transpose(bank[b][:, c * SP:c * SP + P], ctx_a[:, b, c * P:(c + 1) * P], ident[:, :])
                    ins = nc.tensor.transpose(bank[b][:, c * SP + P:c * SP + S], ctx_b[:, b, c * P:(c + 1) * P], ident[0:S2, 0:S2])
                ins.then_inc(setup_filled, 1)
            pe.wait_ge(w_loaded, 64)
            for n, which in ((2, 1), (3, 2), (4, 0), (5, 3)):
                for c in range(KC):
                    for o in range(KC):
                        ins = nc.tensor.transpose(bank[n][:, c * D + o * P:c * D + (o + 1) * P], W_nat[:, which, o, c * P:(c + 1) * P], ident[:, :])
                ins.then_inc(setup_filled, 1)
            pe.wait_ge(bias_loaded, 16 * BIAS_DMAS)
            nc.tensor.transpose(bank[6][:, 0:E * FC], b1_nat[:, :], ident[0:E * FC, 0:E * FC]).then_inc(setup_filled, 1)
            pe.wait_ge(setup_evac_act, 4)
            pe.wait_ge(setup_evac_dve, 3)
            for c in range(KC):
                for k in range(KC):
                    ins = nc.tensor.matmul(bank[c][:, 0:B * S].rearrange("p (b s) -> p b s", b=B), WT_kv[:, 0, k, c * P:(c + 1) * P], ctxT[:, k, :, 0:S],
                                           start=(k == 0), stop=(k == KC - 1))
                ins.then_inc(kv_filled, 1)
            for b in range(B):
                for k in range(KC):
                    ins = nc.tensor.matmul(bank[2][:, b * D:(b + 1) * D], ctxT[:, k, b, 0:P], WT_kv[:, 1, k, :], start=(k == 0), stop=(k == KC - 1))
            ins.then_inc(kv_filled, 1)
            pe.wait_ge(ctx_late_made, 1)
            for b in range(B):
                for k in range(KC):
                    ins = nc.tensor.matmul(bank[3][:, b * D:(b + 1) * D], ctxT_late[:, k, b, :, :].rearrange("p j s -> p (j s)"),
                                           WT_kv[:, 1, k, :], start=(k == 0), stop=(k == KC - 1))
            ins.then_inc(kv_filled, 1)

            def a_use(kind, v):
                n = a_nth[kind, v]
                if n >= 2:
                    pe.wait_ge(a_evac, n - 1)

            def q_use(kind, v):
                n = q_nth[kind, v]
                if n >= 2:
                    pe.wait_ge(q_free, n - 1)

            def softmax_v(g):
                u, i = divmod(g, ITEMS)
                kind, n = item_heads(i)
                b = u // UNITS_PER_BATCH
                pe.wait_ge(exp_done, g + 1)
                if i == 0:
                    if u >= 1:
                        pe.wait_ge(attn_normed, 2 * u)
                    else:
                        pe.wait_ge(v_made, 2)
                for j in range(2):
                    for a in range(2):
                        lhs = probs[:, g % 3, a, j * P:(j + 1) * P]
                        if kind == "pair":
                            h = 2 * n + a
                            dst, rhs = PV_BANKS[j][:, h * (HD + 1):(h + 1) * (HD + 1)], v_a[:, b, h, :]
                        else:
                            q = 2 * n + a
                            dst, rhs = PV_BANKS[j][:, 4 * q * (HD + 1):4 * (q + 1) * (HD + 1)], v_b[:, b, q, :, :].rearrange("p j d -> p (j d)")
                        ins = nc.tensor.matmul(dst, lhs, rhs, start=(i == 0 and a == 0), stop=(kind == "late"), skip_group_check=True)
                ins.then_inc(pv_done, 1)

            def max_scores(v, n):
                b = v // UNITS_PER_BATCH
                g = 2 * NPAIR * v + n
                j, p = divmod(n, NPAIR)
                if n == 0:
                    pe.wait_ge(qst_landed[v % 3], QST_PER_USE * (v // 3 + 1))
                    if v == 0:
                        pe.wait_ge(kst_landed, KST_LANDED)
                        pe.wait_ge(kst_mid_landed, KST_MID_LANDED)
                        pe.wait_ge(mask_row_made, B)
                if g >= 2:
                    pe.wait_ge(rowmax_done, g - 1)
                nc.tensor.matmul(S1_BANKS[g % 2][:, 0:2 * S].rearrange("p (a s) -> p a s", a=2), qst[v % 3][0:ROW_MAX, p, j * P:(j + 1) * P],
                                 kst[0:ROW_MAX, b, p, :, 0:S], start=True, stop=True).then_inc(s1_filled, 1)

            for u in FRAMES:
                for i in range(ITEMS):
                    if i == 0 and live(u - 1):
                        softmax_v(ITEMS * u - 1)
                    if live(u):
                        g = ITEMS * u + i
                        b = u // UNITS_PER_BATCH
                        kind, n = item_heads(i)
                        if g >= 2:
                            pe.wait_ge(exp_done, g - 1)
                        if i == 0:
                            pe.wait_ge(max_landed[u % 3], MAX_PER_USE * (u // 3 + 1))
                        if g == 4:
                            pe.wait_ge(kst_late_made, 1)
                        dst = S2_BANKS[g % 2]
                        if kind == "pair":
                            for a in range(2):
                                ins = nc.tensor.matmul(dst[:, a * UT:(a + 1) * UT], kst[0:ROWS, b, n, a, 0:P], qst[u % 3][0:ROWS, n, :],
                                                       start=True, stop=True)
                        else:
                            for p in range(4 * n, 4 * n + 4):
                                half, q = p % 2, (p // 2) % 2
                                ins = nc.tensor.matmul(dst[64 * half:64 * half + 64, q * UT:(q + 1) * UT], kst_late[0:ROWS, b, p, :],
                                                       qst[u % 3][0:ROWS, p, :], start=True, stop=True)
                        ins.then_inc(s2_filled, 1)
                    n = MAX_ITEMS * i
                    if live(u + 1):
                        for m in range(n, min(n + 2, 2 * NPAIR)):
                            max_scores(u + 1, m)
                    if i >= 1 and live(u):
                        softmax_v(ITEMS * u + i - 1)
                    if live(u + 1):
                        for m in range(n + 2, min(n + MAX_ITEMS, 2 * NPAIR)):
                            max_scores(u + 1, m)
                    if i == 0 and live(u + 2):
                        v = u + 2
                        a_use("xT", v)
                        pe.wait_ge(ln1_done, v + 1)
                        for c in range(KC):
                            for j in range(2):
                                ins = nc.tensor.transpose(A_BANK[:, c * UT + j * P:c * UT + (j + 1) * P], xn[:, j, c * P:(c + 1) * P], ident[:, :])
                        ins.then_inc(a_filled, 1)
                    if i == 1 and live(u + 2):
                        v = u + 2
                        q_use("q", v)
                        pe.wait_ge(a_evac, a_nth["xT", v])
                        for c in range(KC):
                            for k in range(KC):
                                ins = nc.tensor.matmul(Q_BANK[:, c * UT:(c + 1) * UT], WT_qo[:, 0, k, c * P:(c + 1) * P], xnT[:, k, :], start=(k == 0), stop=(k == KC - 1))
                        ins.then_inc(q_filled, 1)
                    if i == 2 and live(u - 1):
                        v = u - 1
                        a_use("attnT", v)
                        pe.wait_ge(attn_normed, 2 * (v + 1))
                        for j in range(2):
                            for c in range(KC):
                                ins = nc.tensor.transpose(A_BANK[:, (j * KC + c) * P:(j * KC + c + 1) * P], attn[:, j, c * P:(c + 1) * P], ident[:, :])
                        ins.then_inc(a_filled, 1)
                    if i == 3 and live(u - 1):
                        v = u - 1
                        q_use("wo", v)
                        pe.wait_ge(a_evac, a_nth["attnT", v])
                        for j in range(2):
                            for c in range(KC):
                                ins = nc.tensor.matmul(Q_BANK[:, j * D:(j + 1) * D], attnT[:, j, c, :], WT_qo[:, 1, c, :], start=(c == 0), stop=(c == KC - 1))
                        ins.then_inc(q_filled, 1)
                    if i == 6 and live(u + 1):
                        v = u + 1
                        a_use("maxT", v)
                        pe.wait_ge(negmax_done, v + 1)
                        nc.tensor.transpose(A_BANK[0:2 * N_HEADS, 0:P], negmax[:, :], ident[:, :]).then_inc(a_filled, 1)
                    if i == 8 and live(u - 1):
                        v = u - 1
                        a_use("xn2T", v)
                        pe.wait_ge(ln2_done, v + 1)
                        for j in range(2):
                            for c in range(KC):
                                ins = nc.tensor.transpose(A_BANK[:, (j * KC + c) * P:(j * KC + c + 1) * P], xn2[:, j, c * P:(c + 1) * P], ident[:, :])
                        ins.then_inc(a_filled, 1)
                    if i == 9 and live(u - 1):
                        v = u - 1
                        q_use("logits", v)
                        pe.wait_ge(a_evac, a_nth["xn2T", v])
                        for j in range(2):
                            for c in range(KC):
                                ins = nc.tensor.matmul(Q_BANK[:, j * E:(j + 1) * E], xn2T[:, j, c, :], wg_sb[:, c, :], start=(c == 0), stop=(c == KC - 1))
                        ins.then_inc(q_filled, 1)

            pe.wait_ge(consts2_made, 5)
            pe.wait_ge(chosen_made, 1)
            nc.tensor.matmul(bank[0][:, 0:T * E], before[:, :], chosen16[:, :], start=True, stop=False, skip_group_check=True)
            for k in range(1, T):
                ins = nc.tensor.matmul(bank[0][:, k * E:T * E], ones[:, :], chosen16[:, 0:(T - k) * E], start=False, stop=(k == T - 1), skip_group_check=True)
            ins.then_inc(ranked, 1)
            for t in range(T):
                ins = nc.tensor.matmul(bank[1][:, 0:E], ones[:, :], chosen16[:, t * E:(t + 1) * E], start=(t == 0), stop=(t == T - 1))
            ins.then_inc(ranked, 1)
            pe.wait_ge(comb_made, 1)
            for t in range(T):
                ins = nc.tensor.transpose(bank[3 + t // 4][0:E, t % 4 * P:(t % 4 + 1) * P], combine[:, t, :], ident[:, :])
                if t % 4 == 3:
                    ins.then_inc(combT_filled, 1)
            for n in range(TOP_K * T):
                if n % PLACES == 0:
                    pe.wait_ge(at_place_made, n // PLACES + 1)
                ins = nc.tensor.matmul(bank[2][:, 0:2 * TAB], at_place[:, n, :], tab_rhs[:, n, :, :].rearrange("p v t -> p (v t)"),
                                       start=(n == 0), stop=(n == TOP_K * T - 1))
            ins.then_inc(tab_filled, 1)
            pe.wait_ge(combT_made, 4)
            for u in range(U):
                if u >= 4:
                    pe.wait_ge(init_added, u - 3)
                for j in range(2):
                    ins = nc.tensor.matmul(INIT_BANKS[u % 4][:, j * D:(j + 1) * D], combineT[:, 2 * u + j, :], b2_sb[:, :], start=True, stop=True)
                ins.then_inc(init_filled, 1)

            def turn(t, par, nth, warm=True):
                pe.wait_ge(gathered[par], nth)
                if warm:
                    pe.wait_ge(xl_made, t - 1)
                for c in range(KC):
                    ins = nc.tensor.transpose(XT_BANKS[par][:, c * P:(c + 1) * P], xg[par][:, c * P:(c + 1) * P], ident[:, :])
                ins.then_inc(xt_filled, 1)

            def weights_of(t):
                return pe.value_load(weight_col[0:1, bass.ds(t, 1)], min_val=0, max_val=(E - 1) * KC * F)

            def layer1(t, par, m, base, warm=True):
                half = m // (FC // 2)
                if warm and m % (FC // 2) == 0:
                    pe.wait_ge(gelu_done, 2 * t + half - 3)
                dst = H_BANKS[par][half][:, m % 4 * P:(m % 4 + 1) * P]
                for c in range(KC):
                    cut = slice(c * P, (c + 1) * P)
                    wh = W1H[:, bass.ds(base + (c * F + m * P), P)]
                    wl = W1L[:, bass.ds(base + (c * F + m * P), P)]
                    nc.tensor.matmul(dst, wh, xh[par][:, cut], start=(c == 0), stop=False)
                    nc.tensor.matmul(dst, wh, xl[par][:, cut], start=False, stop=False)
                    ins = nc.tensor.matmul(dst, wl, xh[par][:, cut], start=False, stop=(c == KC - 1))
                if m % (FC // 2) == FC // 2 - 1:
                    ins.then_inc(h_filled, 1)

            def layer2(t, par, m, base, warm=True):
                if warm and m == 0:
                    pe.wait_ge(y_made, t - 1)
                if m % (FC // 2) == 0:
                    pe.wait_ge(hl_made, 2 * t + m // (FC // 2) + 1)
                cut = slice(m * P, (m + 1) * P)
                both = W2[:, :, bass.ds(base + m * D, D)]
                nc.tensor.matmul(Y_BANKS[par][:, :].rearrange("p (v d) -> p v d", v=2), hh[par][:, cut], both,
                                 start=(m == 0), stop=(m == FC - 1), skip_group_check=True)
                ins = nc.tensor.matmul(Y_BANKS[par][:, 0:D], hl[par][:, cut], both[:, 0, :], start=False, stop=(m == FC - 1), skip_group_check=True)
                if m == FC - 1:
                    ins.then_inc(y_filled, 1)

            def both_layers(t, par, base, next_base, warm1=True, warm2=True):
                pe.wait_ge(xl_made, t + 2)
                for m in range(FC):
                    layer1(t + 1, 1 - par, m, next_base, warm=warm1)
                    layer2(t, par, m, base, warm=warm2)

            turn(0, 0, 16, warm=False)
            turn(1, 1, 16, warm=False)
            pe.wait_ge(init_added, U)
            pe.wait_ge(w_ready, len(chunks))
            first, second = weights_of(0), weights_of(1)
            pe.wait_ge(xl_made, 1)
            for m in range(FC):
                layer1(0, 0, m, first, warm=False)
            turn(2, 0, 32)
            both_layers(0, 0, first, second, warm1=False, warm2=False)

            weights_carried = pe.alloc_register("weights_carried")

            def two_tiles(t, base, first=False):
                turn(t + 2, 1, 8 * (t + 1) + 16)
                next_base = weights_of(t + 1)
                both_layers(t, 1, base, next_base, warm2=not first)
                turn(t + 3, 0, 8 * (t + 1) + 32)
                last_base = weights_of(t + 2)
                both_layers(t + 1, 0, next_base, last_base)
                pe.reg_mov(weights_carried, last_base)

            two_tiles(1, second, first=True)
            with pe.Fori(0, LOOP) as pair:
                two_tiles(pair * 2 + 3, pe.snap(weights_carried, min_val=0, max_val=(E - 1) * KC * F))
            bases = [weights_of(NT - 2), weights_of(NT - 1)]
            both_layers(NT - 2, 1, bases[0], bases[1])
            for m in range(FC):
                layer2(NT - 1, 0, m, bases[1])


_INS = ["x", "ctx_1024", "mask_BxS2_bf1", "g_xattn", "g_ffn", "L0_xattn_Wq", "L0_xattn_bq", "L0_xattn_Wk", "L0_xattn_bk",
        "L0_xattn_Wv", "L0_xattn_bv", "L0_xattn_Wo", "L0_xattn_bo", "L0_ffn_Wg", "L0_ffn_W1", "L0_ffn_b1", "L0_ffn_W2", "L0_ffn_b2"]


def kernel(**inputs):
    import numpy as _np
    import concourse.bacc as _bacc
    from concourse import mybir as _mybir
    from concourse.bass_utils import run_bass_kernel_spmd as _run

    nc = _bacc.Bacc("TRN2", target_bir_lowering=False, num_devices=1)
    arrays, args = {}, []
    for name in _INS:
        a = _np.ascontiguousarray(inputs[name])
        if a.dtype == _np.bool_:
            a = a.view(_np.uint8)
        arrays[f"in_{name}"] = a
        args.append(nc.dram_tensor(f"in_{name}", a.shape, _mybir.dt.from_np(a.dtype), kind="ExternalInput").ap())
    B, L, D = inputs["x"].shape
    args.append(nc.dram_tensor("out_rows", (B * L + P, D), _mybir.dt.float32, kind="ExternalOutput").ap())
    build(nc, *args)
    r = _run(nc, [arrays], core_ids=[0])
    return r.results[0]["out_rows"][0:B * L].reshape(B, L, D)
```
